# Optimizing a Trainium2 kernel written in Bass

```python
import numpy as np
import jax
import jax.numpy as jnp

def _softmax(x, axis=-1):
    return jax.nn.softmax(x, axis=axis)

def _gelu(x):
    return jax.nn.gelu(x, approximate=True)

def _silu(x):
    return jax.nn.silu(x)

def _sigmoid(x):
    return jax.nn.sigmoid(x)

def _layernorm(x, axis=-1, eps=1e-05):
    m = jnp.mean(x, axis=axis, keepdims=True)
    v = jnp.var(x, axis=axis, keepdims=True)
    return (x - m) / jnp.sqrt(v + eps)

def _scatter_add(tgt, idx, src, axis=0):
    return tgt.at[idx].add(src)

def _segment_sum(src, seg, n):
    return jax.ops.segment_sum(src, seg, n)
kernel_name = 'mk_seq_postln_d1_jaxref_r8_8c2ba1'

def setup_inputs(seed: int=0):
    np.random.seed(seed)
    _w = jnp.asarray

    def _L0_attn_setup():
        import jax, jax.numpy as jnp
        import numpy as np
        DIM = 128
        HEADS = 16
        DIM_HEAD = 64
        SOFTCLAMP = 50.0

        def _rmsnorm(x, w):
            eps = jnp.finfo(x.dtype).eps
            var = jnp.mean(jnp.square(x), axis=-1, keepdims=True)
            return x * jax.lax.rsqrt(var + eps) * w

        def _head_rmsnorm(x, gamma):
            norm = jnp.linalg.norm(x, axis=-1, keepdims=True)
            normed = x / jnp.maximum(norm, 1e-12)
            scale = (gamma + 1.0) * DIM_HEAD ** 0.5
            return normed * scale[None, :, None, :]
        key = jax.random.key(seed)
        ks = jax.random.split(key, 7)
        b, n = (4, 256)
        di = HEADS * DIM_HEAD
        s = 0.02
        return {'tokens': jax.random.normal(ks[0], (b, n, DIM), dtype=jnp.float32), 'norm_w': jnp.ones((DIM,), dtype=jnp.float32), 'Wq': jax.random.normal(ks[1], (DIM, di), dtype=jnp.float32) * s, 'Wkv': jax.random.normal(ks[2], (DIM, 2 * di), dtype=jnp.float32) * s, 'Wo': jax.random.normal(ks[3], (di, DIM), dtype=jnp.float32) * s, 'q_gamma': jnp.zeros((HEADS, DIM_HEAD), dtype=jnp.float32), 'k_gamma': jnp.zeros((HEADS, DIM_HEAD), dtype=jnp.float32)}
    _L0_attn_in = _L0_attn_setup()

    def _L0_ffn_setup():
        import jax, jax.numpy as jnp
        import numpy as np
        B, T, D, F, E = (2, 128, 128, 512, 8)
        EPS = 1e-06
        key = jax.random.key(seed)
        k = jax.random.split(key, 5)
        scale = 0.02
        return {'x': jax.random.normal(k[0], (B, T, D), dtype=jnp.float32), 'rms_w': jnp.ones((D,), dtype=jnp.float32), 'gate_w': jax.random.normal(k[1], (E, D), dtype=jnp.float32) * scale, 'W1': jax.random.normal(k[2], (E, D, F), dtype=jnp.float32) * scale, 'b1': jnp.zeros((E, F), dtype=jnp.float32), 'W2': jax.random.normal(k[3], (E, F, D), dtype=jnp.float32) * scale, 'b2': jnp.zeros((E, D), dtype=jnp.float32)}
    _L0_ffn_in = _L0_ffn_setup()
    _d = {'L0_attn_tokens': _L0_attn_in['tokens'], 'L0_attn_norm_w': _L0_attn_in['norm_w'], 'L0_attn_Wq': _L0_attn_in['Wq'], 'L0_attn_Wkv': _L0_attn_in['Wkv'], 'L0_attn_Wo': _L0_attn_in['Wo'], 'L0_attn_q_gamma': _L0_attn_in['q_gamma'], 'L0_attn_k_gamma': _L0_attn_in['k_gamma'], 'L0_ffn_rms_w': _L0_ffn_in['rms_w'], 'L0_ffn_gate_w': _L0_ffn_in['gate_w'], 'L0_ffn_W1': _L0_ffn_in['W1'], 'L0_ffn_b1': _L0_ffn_in['b1'], 'L0_ffn_W2': _L0_ffn_in['W2'], 'L0_ffn_b2': _L0_ffn_in['b2']}
    _x0 = _d['L0_attn_tokens']
    _d['L0_attn_tokens'] = jax.random.normal(jax.random.fold_in(jax.random.key(seed), 1), (8, 512, 128), dtype=_x0.dtype)
    del _x0
    return _d

def reference(L0_attn_tokens, L0_attn_norm_w, L0_attn_Wq, L0_attn_Wkv, L0_attn_Wo, L0_attn_q_gamma, L0_attn_k_gamma, L0_ffn_rms_w, L0_ffn_gate_w, L0_ffn_W1, L0_ffn_b1, L0_ffn_W2, L0_ffn_b2):

    def _L0_attn_ref(tokens, norm_w, Wq, Wkv, Wo, q_gamma, k_gamma):
        import jax, jax.numpy as jnp
        import numpy as np
        DIM = 128
        HEADS = 16
        DIM_HEAD = 64
        SOFTCLAMP = 50.0

        def _rmsnorm(x, w):
            eps = jnp.finfo(x.dtype).eps
            var = jnp.mean(jnp.square(x), axis=-1, keepdims=True)
            return x * jax.lax.rsqrt(var + eps) * w

        def _head_rmsnorm(x, gamma):
            norm = jnp.linalg.norm(x, axis=-1, keepdims=True)
            normed = x / jnp.maximum(norm, 1e-12)
            scale = (gamma + 1.0) * DIM_HEAD ** 0.5
            return normed * scale[None, :, None, :]
        b, n, _ = tokens.shape
        x = _rmsnorm(tokens, norm_w)
        q = x @ Wq
        kv = x @ Wkv
        k, v = jnp.split(kv, 2, axis=-1)
        split = lambda t: t.reshape(b, n, HEADS, DIM_HEAD).transpose(0, 2, 1, 3)
        q, k, v = (split(q), split(k), split(v))
        q = _head_rmsnorm(q, q_gamma)
        k = _head_rmsnorm(k, k_gamma)
        sim = jnp.einsum('bhid,bhjd->bhij', q, k)
        sim = jnp.tanh(sim / SOFTCLAMP) * SOFTCLAMP
        sim = sim * DIM_HEAD ** (-0.5)
        attn = jax.nn.softmax(sim, axis=-1)
        out = jnp.einsum('bhij,bhjd->bhid', attn, v)
        out = out.transpose(0, 2, 1, 3).reshape(b, n, HEADS * DIM_HEAD)
        return out @ Wo

    def _L0_ffn_ref(x, rms_w, gate_w, W1, b1, W2, b2):
        import jax, jax.numpy as jnp
        import numpy as np
        B, T, D, F, E = (2, 128, 128, 512, 8)
        EPS = 1e-06
        ms = jnp.mean(x * x, axis=-1, keepdims=True)
        xn = x * jax.lax.rsqrt(ms + EPS) * rms_w
        logits = jnp.einsum('btd,ed->bte', xn, gate_w)
        scores = jax.nn.softmax(logits, axis=-1)
        top1_idx = jnp.argmax(scores, axis=-1)
        top1_score = jnp.max(scores, axis=-1)
        out = jnp.zeros_like(xn)
        for e in range(E):
            h = jax.nn.silu(jnp.einsum('btd,df->btf', xn, W1[e]) + b1[e])
            ye = jnp.einsum('btf,fd->btd', h, W2[e]) + b2[e]
            out = jnp.where((top1_idx == e)[..., None], ye, out)
        return out * top1_score[..., None]
    x = L0_attn_tokens
    x = _layernorm(x + _L0_attn_ref(x, L0_attn_norm_w, L0_attn_Wq, L0_attn_Wkv, L0_attn_Wo, L0_attn_q_gamma, L0_attn_k_gamma), axis=-1)
    x = _layernorm(x + _L0_ffn_ref(x, L0_ffn_rms_w, L0_ffn_gate_w, L0_ffn_W1, L0_ffn_b1, L0_ffn_W2, L0_ffn_b2), axis=-1)
    return x

_drawn_inputs = setup_inputs


def setup_inputs(seed=0):
    import zlib

    import numpy as np

    out = dict(_drawn_inputs(seed))
    spreads = {'L0_attn_norm_w': (1.0, 0.6),
     'L0_attn_q_gamma': (0.0, 0.8),
     'L0_attn_k_gamma': (0.0, 0.8),
     'L0_ffn_rms_w': (1.0, 0.6),
     'L0_ffn_b1': (0.0, 0.8),
     'L0_ffn_b2': (0.0, 0.462)}
    factors = {'L0_attn_Wq': 3.633,
     'L0_attn_Wkv': 3.375,
     'L0_attn_Wo': 3.375,
     'L0_ffn_gate_w': 3.023,
     'L0_ffn_W1': 5.926,
     'L0_ffn_W2': 5.467}
    for name, (base, spread) in spreads.items():
        noise = np.random.default_rng([zlib.crc32(name.encode()), seed]).standard_normal(out[name].shape)
        drawn = base * np.exp(spread * noise) if base else spread * noise
        out[name] = jnp.asarray(drawn.astype(out[name].dtype))
    for name, factor in factors.items():
        out[name] = (out[name] * factor).astype(out[name].dtype)
    return out
```

```python
from contextlib import ExitStack

import concourse.bass as bass
import concourse.mybir as mybir

F32 = mybir.dt.float32
F32R = mybir.dt.float32r
I32 = mybir.dt.int32
ALU = mybir.AluOpType
ACT = mybir.ActivationFunctionType
AX_X = mybir.AxisListType.X

P = 128
D = 128
HEADS, DH = 16, 64
BATCHES, SEQ = 8, 512
TOKENS = BATCHES * SEQ
PAIRS = HEADS // 2
GROUPS = BATCHES * PAIRS
QT = SEQ // P
TILES = TOKENS // P
EXPERTS, FF = 8, 512
FK = FF // P
SLOT_TILES = TILES + EXPERTS - 1
DRAM_TILES = EXPERTS * TILES + EXPERTS - 1
ZERO_TILES = 32
ZEROS_STORED = 16 * -(-DRAM_TILES // ZERO_TILES)
CLAMP = 50.0
EPS_ATTN = 1.1920928955078125e-07
EPS_FFN = 1e-6
EPS_LN = 1e-5
TINY = 1e-24
RSQRT_MAGIC = float(0x5F3759DF)


class Steps:

    def __init__(self, engine, sem):
        self.engine, self.sem, self.n = engine, sem, 0

    def restart(self):
        self.engine.sem_clear(self.sem)
        self.n = 0

    def after(self, instruction):
        instruction.then_inc(self.sem, 1)
        self.n += 1
        self.engine.wait_ge(self.sem, self.n)


def build(nc, tokens, norm_w, wq, wkv, wo, q_gamma, k_gamma, rms_w, gate_w, w1, b1, w2, b2, out):
    sorted_x = nc.dram_tensor("sorted_x", [DRAM_TILES * P, D], F32, kind="Internal").ap()
    sorted_y = nc.dram_tensor("sorted_y", [SLOT_TILES * P, D], F32, kind="Internal").ap()

    with ExitStack() as ctx:
        def sb(name, shape, dt=F32):
            return ctx.enter_context(nc.sbuf_tensor(name, shape, dt))

        def sem(name):
            return ctx.enter_context(nc.semaphore(name))

        w_hi = sb("w_hi", [P, PAIRS, 3 * P], F32R)
        w_lo = sb("w_lo", [P, PAIRS, 3 * P], F32R)
        w_o = sb("w_o", [P, PAIRS, D])
        w_1 = sb("w_1", [P, EXPERTS, FF])
        w_2 = sb("w_2", [P, EXPERTS, FK * D])
        b_1 = sb("b_1", [P, EXPERTS, FF])
        b_2 = sb("b_2", [P, EXPERTS, D])
        gate_t = sb("gate_t", [P, EXPERTS])
        norm_col = sb("norm_col", [P, 1])
        rms_col = sb("rms_col", [P, 1])
        gam = sb("gam", [P, 2, PAIRS])
        scale_qk = sb("scale_qk", [P, 2, PAIRS])
        ident = sb("ident", [P, P])
        ones = sb("ones", [P, P])
        before = sb("before", [P, P])
        count_i = sb("count_i", [P, 64], I32)
        count = sb("count", [P, 64])
        tile_starts = sb("tile_starts", [P, TILES])
        first_slots = sb("first_slots", [P, EXPERTS])
        carry = sb("carry", [P, EXPERTS, QT])
        zeros = b_1[:].rearrange("p e f -> p (e f)")

        x = sb("x", [P, TILES, D])
        xh = sb("xh", [P, QT, D])
        xq = sb("xq", [P, QT, D])
        xt_hi = sb("xt_hi", [P, SEQ], F32R)
        xt_lo = sb("xt_lo", [P, SEQ], F32R)
        sq = sb("sq", [P, 4, 2 * P])
        qk = sb("qk", [P, QT, 2 * P])
        qt_hi = sb("qt_hi", [P, 2, SEQ], F32R)
        qt_lo = sb("qt_lo", [P, 2, SEQ], F32R)
        kt_hi = sb("kt_hi", [P, 2, SEQ], F32R)
        kt_lo = sb("kt_lo", [P, 2, SEQ], F32R)
        v = sb("v", [P, 4, QT, P])
        pr = sb("pr", [P, 2, QT, 2 * SEQ])
        part = sb("part", [P, 2, 2 * SEQ])
        sums = sb("sums", [P, 2 * SEQ])
        den_t = sb("den_t", [P, SEQ])
        den_r = sb("den_r", [P, SEQ // 32])
        at = sb("at", [P, PAIRS, SEQ])
        xrt = sb("xrt", [P, SEQ])
        ss = sb("ss", [P, 64])
        rs = sb("rs", [P, 64])
        na = sb("na", [P, 64])
        stats = sb("stats", [P, QT, 6])
        mv = sb("mv", [P, QT, 2])
        nb = sb("nb", [P, 64])

        logits = sb("logits", [P, TILES, EXPERTS])
        top = sb("top", [P, TILES])
        is_top = sb("is_top", [P, QT, EXPERTS])
        choice = sb("choice", [P, QT, EXPERTS])
        least = sb("least", [P, QT])
        hot = sb("hot", [P, EXPERTS, QT])
        batch_logits = sb("batch_logits", [P, QT, EXPERTS])
        ranks = sb("ranks", [P, 2, EXPERTS, QT])
        tot = ranks[:, 1, :, :]
        incl = sb("incl", [P, EXPERTS, QT])
        rank = sb("rank", [P, EXPERTS, QT])
        slot_f = sb("slot_f", [P, QT])
        batch_slot = sb("batch_slot", [P, QT], I32)
        next_slot = sb("next_slot", [P, EXPERTS])
        slot = sb("slot", [P, TILES], I32)
        score = sb("score", [P, TILES])
        row_f = sb("row_f", [P, TILES])
        row = sb("row", [P, TILES], I32)
        n_tiles = sb("n_tiles", [P, EXPERTS])
        ends = sb("ends", [P, EXPERTS])
        owner_f = sb("owner_f", [P, SLOT_TILES])
        owner = sb("owner", [P, SLOT_TILES], I32)
        place_f = sb("place_f", [P, SLOT_TILES])
        place = sb("place", [P, SLOT_TILES], I32)
        ra, rb = at[:, 0, 0:TILES * EXPERTS], at[:, 0, TILES * EXPERTS:2 * TILES * EXPERTS]
        cmp_s = at[:, 4, 0:SLOT_TILES * EXPERTS].rearrange("p (s e) -> p s e", e=EXPERTS)
        cmp_n = at[:, 5, 0:SLOT_TILES * EXPERTS].rearrange("p (s e) -> p s e", e=EXPERTS)

        w_f = pr[:, 1, :, :].rearrange("p a b -> p (a b)")[:, 0:PAIRS * 3 * P].rearrange("p (c n) -> p c n", c=PAIRS)

        p0 = pr[:, 0, :, :].rearrange("p a b -> p (a b)")
        p1 = pr[:, 1, :, :].rearrange("p a b -> p (a b)")
        pre = [p0[:, m * FF:(m + 1) * FF] for m in range(3)]
        th = [p0[:, (3 + m) * FF:(4 + m) * FF] for m in range(3)]
        ht_sb = p0[:, 6 * FF:7 * FF]
        hid = [p1[:, m * FF:(m + 1) * FF] for m in range(3)]
        xs = [p1[:, 3 * FF + m * P:3 * FF + (m + 1) * P] for m in range(3)]
        xst = [p1[:, 3 * FF + (3 + m) * P:3 * FF + (4 + m) * P] for m in range(3)]
        ys = [p1[:, 3 * FF + (6 + m) * P:3 * FF + (7 + m) * P] for m in range(3)]
        yr = pr[:].rearrange("p a b c -> p (a b c)")[:, 0:TILES * D].rearrange("p (t d) -> p t d", d=D)

        ps = ctx.enter_context(nc.psum_tensor("ps", [P, 8, 512], F32))
        S = [ps[:, 2 * k:2 * k + 2, :] for k in range(2)]
        AV, DEN, XA, XB = ps[:, 4, :], ps[:, 5, :], ps[:, 6, :], ps[:, 7, :]
        U = [ps[:, m, :] for m in range(3)]
        HT, Y, XST = ps[:, 3, :], ps[:, 4, 0:D], ps[:, 5, 0:P]

        x0_loaded, x_loaded = sem("x0_loaded"), sem("x_loaded")
        w_first_loaded, w_loaded, cols_loaded = sem("w_first_loaded"), sem("w_loaded"), sem("cols_loaded")
        wo_loaded, ffn_loaded = sem("wo_loaded"), sem("ffn_loaded")
        w_split = sem("w_split")
        zeroed = sem("zeroed")
        zeros_stored = sem("zeros_stored")
        made, consts_ready, scale_ready = sem("made"), sem("consts_ready"), sem("scale_ready")
        dve_steps, pool_steps = sem("dve_steps"), sem("pool_steps")
        xh_ready, xt_transposed = sem("xh_ready"), sem("xt_transposed")
        xt_hi_ready, xt_ready = sem("xt_hi_ready"), sem("xt_ready")
        qk_projected = sem("qk_projected")
        squared, qk_scaled = sem("squared"), sem("qk_scaled")
        squares_summed = sem("squares_summed")
        v_projected, v_copied = sem("v_projected"), sem("v_copied")
        q_transposed, qt_hi_ready, qt_ready = sem("q_transposed"), sem("qt_hi_ready"), sem("qt_ready")
        k_transposed, kt_hi_ready, kt_ready = sem("k_transposed"), sem("kt_hi_ready"), sem("kt_ready")
        scored, tanh_done, exp_done = sem("scored"), sem("tanh_done"), sem("exp_done")
        pv_done, sums_ready, den_done, at_ready = sem("pv_done"), sem("sums_ready"), sem("den_done"), sem("at_ready")
        wo_done, x1_ready = sem("wo_done"), sem("x1_ready")
        xq_ready, xq_transposed, xrt_ready = sem("xq_ready"), sem("xq_transposed"), sem("xrt_ready")
        logits_done, logits_copied = sem("logits_done"), sem("logits_copied")
        hot_ready, ranked, ranks_copied = sem("hot_ready"), sem("ranked"), sem("ranks_copied")
        slots_ready = sem("slots_ready")
        next_slot_ready, xq_free = sem("next_slot_ready"), sem("xq_free")
        scattered = sem("scattered")
        rows_known = sem("rows_known")
        owners_ready, shifted_ready, score_exp_done = sem("owners_ready"), sem("shifted_ready"), sem("score_exp_done")
        xs_loaded = [sem(f"xs_loaded{m}") for m in range(3)]
        y_stored = [sem(f"y_stored{m}") for m in range(3)]
        xs_transposed, xst_ready, up_done = sem("xs_transposed"), sem("xst_ready"), sem("up_done")
        pre_ready, th_ready, hid_ready = sem("pre_ready"), sem("th_ready"), sem("hid_ready")
        h_transposed, ht_copied, down_done, y_ready = sem("h_transposed"), sem("ht_copied"), sem("down_done"), sem("y_ready")
        gathered = [sem(f"gathered{n}") for n in range(TILES // QT)]
        out_ready, out_stored = sem("out_ready"), sem("out_stored")

        block = ctx.enter_context(nc.Block())

        LEAD = 4
        ROUNDS = BATCHES - 1

        def total(i, k, each, plus):
            n = each * k + plus
            return n if i is None else i * (each * PAIRS) + n

        def batch(i, k, plus=0):
            n = k // PAIRS + plus
            return n if i is None else i + n

        @block.sync
        def _(sp):
            xv = tokens.rearrange("(t p) d -> p t d", p=P)
            sp.dma_start(x[:, 0:QT, :], xv[:, 0:QT, :]).then_inc(x0_loaded, 16)
            for n, w in enumerate((wq, wkv[:, 0:HEADS * DH], wkv[:, HEADS * DH:2 * HEADS * DH])):
                sp.dma_start(w_f[:, 0, n * P:(n + 1) * P], w[:, 0:P]).then_inc(w_first_loaded, 16)
            sp.dma_start(norm_col[:], norm_w).then_inc(cols_loaded, 16)
            sp.dma_start(gam[:, 0, :], q_gamma).then_inc(cols_loaded, 16)
            sp.dma_start(gam[:, 1, :], k_gamma).then_inc(cols_loaded, 16)
            sp.dma_start(rms_col[:], rms_w).then_inc(cols_loaded, 16)
            for n, w in enumerate((wq, wkv[:, 0:HEADS * DH], wkv[:, HEADS * DH:2 * HEADS * DH])):
                sp.dma_start(w_f[:, 1:PAIRS, n * P:(n + 1) * P],
                             w[:, P:PAIRS * P].rearrange("d (c n) -> d c n", n=P)).then_inc(w_loaded, 16)
            sp.dma_start(x[:, QT:TILES, :], xv[:, QT:TILES, :]).then_inc(x_loaded, 16)
            sp.dma_start(w_o[:], wo.rearrange("(c p) n -> p c n", p=P)).then_inc(wo_loaded, 16)
            sp.dma_start(gate_t[:], gate_w).then_inc(wo_loaded, 16)
            sp.wait_ge(zeroed, 1)
            zv = sorted_x.rearrange("(p t) d -> p (t d)", p=P)
            for t in range(0, DRAM_TILES, ZERO_TILES):
                n = min(ZERO_TILES, DRAM_TILES - t) * D
                sp.dma_start(zv[:, t * D:t * D + n], zeros[:, 0:n]).then_inc(zeros_stored, 16)
            sp.dma_start(w_1[:], w1.rearrange("e d f -> d e f")).then_inc(ffn_loaded, 16)
            sp.dma_start(w_2[:].rearrange("p e (k n) -> p (e k) n", k=FK),
                         w2.rearrange("e (k p) n -> p (e k) n", p=P)).then_inc(ffn_loaded, 16)
            sp.wait_ge(zeros_stored, ZEROS_STORED)
            sp.dma_start(b_1[:].rearrange("p e f -> p (e f)"), b1.to_broadcast([P, EXPERTS * FF])).then_inc(ffn_loaded, 16)
            sp.dma_start(b_2[:].rearrange("p e f -> p (e f)"), b2.to_broadcast([P, EXPERTS * D])).then_inc(ffn_loaded, 16)

            def load(s, m):
                t = sp.value_load(place[0:1, bass.ds(s, 1)], min_val=0, max_val=DRAM_TILES - 1)
                sp.dma_start(xs[m % 3], sorted_x[bass.ds(t * P, P), :]).then_inc(xs_loaded[m % 3], 16)

            sp.wait_ge(owners_ready, 1)
            sp.wait_ge(scattered, 16 * TILES)
            for m in range(3):
                load(m, m)
            with sp.Fori(1, SLOT_TILES // 3) as i:
                for m in range(3):
                    sp.wait_ge(xs_transposed, i * 3 + m - 2)
                    load(i * 3 + m, m)
            ov = out.rearrange("(t p) d -> p t d", p=P)
            for n in range(TILES // QT):
                sp.wait_ge(out_ready, n + 1)
                sp.dma_start(ov[:, QT * n:QT * (n + 1), :], yr[:, QT * n:QT * (n + 1), :]).then_inc(out_stored, 16)
            sp.wait_ge(out_stored, 16 * (TILES // QT))

        @block.gpsimd
        def _(pool):
            steps = Steps(pool, pool_steps)
            nc.gpsimd.memset(ident[:], 0.0).then_inc(made, 1)
            nc.gpsimd.memset(ones[:], 1.0).then_inc(made, 1)
            nc.gpsimd.iota(count_i[:], pattern=[[1, 64]], base=0, channel_multiplier=0).then_inc(made, 1)
            pool.wait_ge(made, 3)
            nc.gpsimd.affine_select(out=ident[:], in_=ident[:], compare_op=ALU.not_equal, fill=1.0, base=0,
                                    pattern=[[-1, P]], channel_multiplier=1).then_inc(consts_ready, 1)
            nc.gpsimd.affine_select(out=before[:], in_=ones[:], compare_op=ALU.is_gt, fill=0.0, base=0,
                                    pattern=[[1, P]], channel_multiplier=-1).then_inc(consts_ready, 1)
            nc.gpsimd.memset(zeros, 0.0).then_inc(zeroed, 1)

            def body(i, k, first=False):
                pair = pr[:, k % 2, :, :]
                pool.wait_ge(exp_done, total(i, k, 2, 1))
                steps.after(nc.gpsimd.tensor_tensor(part[:, 0, :], pair[:, 0, :], pair[:, 1, :], ALU.add))
                pool.wait_ge(exp_done, total(i, k, 2, 2))
                steps.after(nc.gpsimd.tensor_tensor(part[:, 1, :], pair[:, 2, :], pair[:, 3, :], ALU.add))
                if not first:
                    pool.wait_ge(den_done, total(i, k, 1, 0))
                nc.gpsimd.tensor_tensor(sums[:], part[:, 0, :], part[:, 1, :], ALU.add).then_inc(sums_ready, 1)
                if k % PAIRS == 3 and k > PAIRS:
                    scatter(batch(i, k))
                pool.wait_ge(sums_ready, total(i, k, 1, 1))

            def scatter(n):
                pool.wait_ge(slots_ready, n)
                nc.gpsimd.tensor_tensor(next_slot[:], next_slot[:], incl[:, :, QT - 1], ALU.add).then_inc(next_slot_ready, 1)
                pool.wait_ge(zeros_stored, ZEROS_STORED)
                for t in range(QT):
                    nc.gpsimd.indirect_dma_start(
                        out=sorted_x, out_offset=bass.IndirectOffsetOnAxis(ap=batch_slot[:, t:t + 1], axis=0),
                        in_=xq[:, t, :], in_offset=None).then_inc(scattered, 16)
                pool.wait_ge(scattered, n * (16 * QT))
                pool.sem_inc(xq_free, 1)

            for k in range(LEAD):
                body(None, k, first=k == 0)
            with pool.Fori(0, ROUNDS) as i:
                steps.restart()
                for k in range(LEAD, LEAD + PAIRS):
                    body(i, k)
            steps.restart()
            for k in range(GROUPS - LEAD, GROUPS):
                body(None, k)
            scatter(BATCHES)
            for m in range(3):
                pool.wait_ge(y_stored[m], 16 * (SLOT_TILES // 3))
            pool.wait_ge(rows_known, 1)
            for t in range(TILES):
                nc.gpsimd.indirect_dma_start(
                    out=yr[:, t, :], out_offset=None, in_=sorted_y,
                    in_offset=bass.IndirectOffsetOnAxis(ap=row[:, t:t + 1], axis=0)).then_inc(gathered[t // QT], 16)

        @block.scalar
        def _(act):
            def squares(i, k, first=False):
                act.wait_ge(qk_projected, total(i, k, 1, 1))
                if not first:
                    act.wait_ge(squares_summed, total(i, k, 1, 0))
                nc.scalar.activation(sq[:].rearrange("p a b -> p (a b)"),
                                     ps[:, 6:8, :].rearrange("p a b -> p (a b)"), ACT.Square).then_inc(squared, 1)

            def copy_v(i, k):
                act.wait_ge(v_projected, total(i, k, 1, 1))
                nc.scalar.activation(v[:, k % 4, :, :].rearrange("p a b -> p (a b)"), XA, ACT.Copy).then_inc(v_copied, 1)

            def tanh(i, k, j):
                act.wait_ge(scored, total(i, k, 4, j + 1))
                nc.scalar.activation(pr[:, k % 2, j, :], S[j % 2].rearrange("p a b -> p (a b)"), ACT.Tanh,
                                     scale=1.0 / CLAMP).then_inc(tanh_done, 1)

            def exps(i, k, half):
                act.wait_ge(tanh_done, total(i, k, 4, 2 * half + 2))
                w = pr[:, k % 2, 2 * half:2 * half + 2, :].rearrange("p a b -> p (a b)")
                nc.scalar.activation(w, w, ACT.Exp, scale=CLAMP / DH ** 0.5).then_inc(exp_done, 1)

            def high(dst, src, scale, done):
                nc.scalar.activation(dst, src, ACT.Copy, scale=scale).then_inc(done, 1)

            def high_q(i, k):
                act.wait_ge(q_transposed, total(i, k, 1, 1))
                high(qt_hi[:, k % 2, :], XB, scale_qk[:, 0, k % PAIRS:k % PAIRS + 1], qt_hi_ready)

            def high_k(i, k):
                act.wait_ge(k_transposed, total(i, k, 1, 1))
                high(kt_hi[:, k % 2, :], XA, scale_qk[:, 1, k % PAIRS:k % PAIRS + 1], kt_hi_ready)

            def high_xt(n):
                act.wait_ge(xt_transposed, n)
                high(xt_hi[:], XB, norm_col[:, 0:1], xt_hi_ready)

            def router_steps(c, n):
                if c == 1:
                    act.wait_ge(xq_transposed, n)
                    high(xrt[:], XB, rms_col[:, 0:1], xrt_ready)
                if c == 2:
                    act.wait_ge(logits_done, n)
                    high(batch_logits[:].rearrange("p a b -> p (a b)"), XB[:, 0:QT * EXPERTS], 1.0, logits_copied)
                if c == 3:
                    act.wait_ge(ranked, n)
                    high(ranks[:].rearrange("p a e t -> p (a e t)"), XB[:, 0:2 * QT * EXPERTS], 1.0, ranks_copied)

            def body(i, k, first=False, prepare=True, score_next=True):
                if score_next:
                    if not first:
                        act.wait_ge(pv_done, total(i, k, 1, 0))
                        act.wait_ge(sums_ready, total(i, k, 1, 0))
                    tanh(i, k + 1, 0)
                if prepare:
                    squares(i, k + 2)
                if score_next:
                    tanh(i, k + 1, 1)
                    exps(i, k + 1, 0)
                    tanh(i, k + 1, 2)
                if prepare:
                    copy_v(i, k + 2)
                if score_next:
                    tanh(i, k + 1, 3)
                if prepare:
                    high_q(i, k + 2)
                    high_k(i, k + 2)
                if score_next:
                    exps(i, k + 1, 1)
                if k >= PAIRS:
                    router_steps(k % PAIRS, batch(i, k))
                if k % PAIRS == 5 and k < GROUPS - LEAD:
                    high_xt(batch(i, k, 2))

            act.wait_ge(cols_loaded, 64)
            high_xt(1)
            act.wait_ge(w_first_loaded, 48)
            high(w_hi[:, 0, :], w_f[:, 0, :], 1.0, w_split)
            act.wait_ge(scale_ready, 1)
            squares(None, 0, first=True)
            copy_v(None, 0)
            high_q(None, 0)
            high_k(None, 0)
            act.wait_ge(w_loaded, 48)
            high(w_hi[:, 1:PAIRS, :], w_f[:, 1:PAIRS, :], 1.0, w_split)
            squares(None, 1)
            tanh(None, 0, 0)
            tanh(None, 0, 1)
            exps(None, 0, 0)
            copy_v(None, 1)
            tanh(None, 0, 2)
            tanh(None, 0, 3)
            high_q(None, 1)
            high_k(None, 1)
            exps(None, 0, 1)
            act.wait_ge(w_split, 4)
            for k in range(LEAD):
                body(None, k, first=k == 0)
            with act.Fori(0, ROUNDS) as i:
                for k in range(LEAD, LEAD + PAIRS):
                    body(i, k)
            for k in range(GROUPS - LEAD, GROUPS):
                body(None, k, prepare=k + 2 < GROUPS, score_next=k + 1 < GROUPS)

            for c in (1, 2, 3):
                router_steps(c, BATCHES)

            def tanh_pre(s, m):
                act.wait_ge(pre_ready, s + 1)
                nc.scalar.activation(th[m % 3], pre[m % 3], ACT.Tanh, scale=0.5).then_inc(th_ready, 1)

            def store(s, m):
                act.wait_ge(y_ready, s + 1)
                act.dma_start(sorted_y[bass.ds(s * P, P), :], ys[m % 3]).then_inc(y_stored[m % 3], 16)

            def tile(s, m, first=False, ahead=True):
                act.wait_ge(h_transposed, s + 1)
                if not first:
                    act.wait_ge(down_done, s)
                nc.scalar.activation(ht_sb, HT, ACT.Copy, scale=0.5).then_inc(ht_copied, 1)
                if ahead:
                    tanh_pre(s + 2, m + 2)
                if not first:
                    store(s - 1, m + 2)

            act.wait_ge(owners_ready, 1)
            tanh_pre(0, 0)
            tanh_pre(1, 1)
            for s in range(3):
                tile(s, s, first=s == 0)
            with act.Fori(1, SLOT_TILES // 3 - 1) as i:
                for m in range(3):
                    tile(i * 3 + m, m)
            for s in range(SLOT_TILES - 3, SLOT_TILES):
                tile(s, s, ahead=s + 2 < SLOT_TILES)
            store(SLOT_TILES - 1, SLOT_TILES - 1)

            act.wait_ge(shifted_ready, 1)
            nc.scalar.activation(rb, ra, ACT.Exp).then_inc(score_exp_done, 1)

        @block.vector
        def _(dve):
            V = nc.vector
            steps = Steps(dve, dve_steps)

            def rsqrt(n):
                y, s, a, b = rs[:, 0:n], ss[:, 0:n], na[:, 0:n], nb[:, 0:n]
                steps.after(V.tensor_scalar(a.bitcast(I32), s.bitcast(I32), 1, None, ALU.logical_shift_right))
                steps.after(V.tensor_scalar(y.bitcast(I32), a.bitcast(I32), -1.0, RSQRT_MAGIC, ALU.mult, ALU.add))
                for _ in range(3):
                    steps.after(V.scalar_tensor_tensor(a, y, -0.5, y, ALU.mult, ALU.mult))
                    steps.after(V.tensor_tensor(b, a, s, ALU.mult))
                    steps.after(V.scalar_tensor_tensor(y, b, 1.5, y, ALU.add, ALU.mult))

            def rows_rms(rows, eps, n=QT):
                tmp = den_t[:].rearrange("p (a b) -> p a b", b=D)
                steps.after(V.tensor_tensor(tmp, rows, rows, ALU.mult))
                steps.after(V.tensor_reduce(ss[:, 0:n], tmp, AX_X, ALU.add))
                steps.after(V.tensor_scalar(ss[:, 0:n], ss[:, 0:n], 1.0 / D, eps, ALU.mult, ALU.add))
                rsqrt(n)

            def centre(rows, n, tmp):
                steps.after(V.tensor_reduce(ss[:, 0:n], rows, AX_X, ALU.add))
                steps.after(V.tensor_scalar(ss[:, 0:n], ss[:, 0:n], 1.0 / D, None, ALU.mult))
                steps.after(V.tensor_tensor(rows, rows, ss[:, 0:n].unsqueeze(2).to_broadcast([P, n, D]), ALU.subtract))
                steps.after(V.tensor_tensor(tmp, rows, rows, ALU.mult))
                steps.after(V.tensor_reduce(ss[:, 0:n], tmp, AX_X, ALU.add))
                steps.after(V.tensor_scalar(ss[:, 0:n], ss[:, 0:n], 1.0 / D, EPS_LN, ALU.mult, ALU.add))
                rsqrt(n)

            def scale_heads(i, k, first=False):
                dve.wait_ge(squared, total(i, k, 1, 1))
                V.tensor_reduce(ss[:, 0:16], sq[:].rearrange("p a (h d) -> p (a h) d", d=DH), AX_X,
                                ALU.add).then_inc(squares_summed, 1)
                dve.wait_ge(squares_summed, total(i, k, 1, 1))
                steps.after(V.tensor_scalar(ss[:, 0:16], ss[:, 0:16], TINY, None, ALU.max))
                rsqrt(16)
                if not first:
                    dve.wait_ge(k_transposed, total(i, k, 1, 0))
                for half, bank in enumerate((XA, XB)):
                    V.tensor_tensor(qk[:, 2 * half:2 * half + 2, :].rearrange("p a (h d) -> p (a h) d", d=DH),
                                    bank.rearrange("p (a d) -> p a d", d=DH),
                                    rs[:, 8 * half:8 * half + 8].unsqueeze(2).to_broadcast([P, 8, DH]),
                                    ALU.mult).then_inc(qk_scaled, 1)

            def low(dst, src, scale, hi, done):
                V.scalar_tensor_tensor(dst, src, scale, hi.bitcast(F32), ALU.mult, ALU.subtract).then_inc(done, 1)

            def low_q(i, k):
                dve.wait_ge(qt_hi_ready, total(i, k, 1, 1))
                low(qt_lo[:, k % 2, :], XB, scale_qk[:, 0, k % PAIRS:k % PAIRS + 1], qt_hi[:, k % 2, :], qt_ready)

            def low_k(i, k):
                dve.wait_ge(kt_hi_ready, total(i, k, 1, 1))
                low(kt_lo[:, k % 2, :], XA, scale_qk[:, 1, k % PAIRS:k % PAIRS + 1], kt_hi[:, k % 2, :], kt_ready)

            def low_xt(n):
                dve.wait_ge(xt_hi_ready, n)
                low(xt_lo[:], XB, norm_col[:, 0:1], xt_hi[:], xt_ready)

            def normalise(i, k):
                dve.wait_ge(den_done, total(i, k, 1, 1))
                steps.after(V.transpose(den_t[:], DEN))
                steps.after(V.reciprocal(den_r[:], den_t[:].rearrange("p (a b) -> p a b", b=32)[:, :, 0]))
                steps.after(V.transpose(den_t[:].rearrange("p (a b) -> p a b", b=32),
                                        den_r[:].unsqueeze(2).to_broadcast([P, SEQ // 32, 32])))
                V.tensor_tensor(at[:, k % PAIRS, :], AV, den_t[:], ALU.mult).then_inc(at_ready, 1)
                dve.wait_ge(at_ready, total(i, k, 1, 1))

            def x_hat(b):
                rows = x[:, bass.ds(b * QT, QT), :]
                rows_rms(rows, EPS_ATTN)
                V.tensor_tensor(xh[:], rows, rs[:, 0:QT].unsqueeze(2).to_broadcast([P, QT, D]),
                                ALU.mult).then_inc(xh_ready, 1)

            def residual(b, n, transposed):
                dve.wait_ge(xt_transposed, transposed)
                dve.wait_ge(wo_done, n)
                V.tensor_tensor(xh[:].rearrange("p a b -> p (a b)"),
                                x[:, bass.ds(b * QT, QT), :].rearrange("p a b -> p (a b)"), DEN,
                                ALU.add).then_inc(x1_ready, 1)

            def layer_norm_1(b, n):
                dve.wait_ge(x1_ready, n)
                centre(xh[:], QT, den_t[:].rearrange("p (a b) -> p a b", b=D))
                steps.after(V.tensor_tensor(x[:, bass.ds(b * QT, QT), :], xh[:],
                                            rs[:, 0:QT].unsqueeze(2).to_broadcast([P, QT, D]), ALU.mult))

            def router_rows(b, n):
                dve.wait_ge(xq_free, n)
                rows = x[:, bass.ds(b * QT, QT), :]
                rows_rms(rows, EPS_FFN)
                V.tensor_tensor(xq[:], rows, rs[:, 0:QT].unsqueeze(2).to_broadcast([P, QT, D]),
                                ALU.mult).then_inc(xq_ready, 1)

            def choose(b, n):
                dve.wait_ge(logits_copied, n)
                lg, tp = logits[:, bass.ds(b * QT, QT), :], top[:, bass.ds(b * QT, QT)]
                steps.after(V.tensor_reduce(least[:], batch_logits[:], AX_X, ALU.max))
                V.tensor_copy(lg, batch_logits[:])
                V.tensor_copy(tp, least[:])
                steps.after(V.tensor_tensor(is_top[:], batch_logits[:], least[:].unsqueeze(2).to_broadcast([P, QT, EXPERTS]),
                                            ALU.is_equal))
                steps.after(V.scalar_tensor_tensor(
                    choice[:], is_top[:], -float(EXPERTS),
                    count[:, 0:EXPERTS].unsqueeze(1).to_broadcast([P, QT, EXPERTS]), ALU.mult, ALU.add))
                steps.after(V.tensor_reduce(least[:], choice[:], AX_X, ALU.min))
                V.tensor_tensor(hot[:].rearrange("p e t -> p t e"), choice[:],
                                least[:].unsqueeze(2).to_broadcast([P, QT, EXPERTS]), ALU.is_equal).then_inc(hot_ready, 1)

            def assign(b, n):
                flat = lambda a: a.rearrange("p e t -> p (e t)")
                dve.wait_ge(next_slot_ready, n)
                dve.wait_ge(ranks_copied, n)
                steps.after(V.tensor_tensor_scan(flat(incl[:]), flat(carry[:]), flat(tot), 0.0, ALU.mult, ALU.add))
                steps.after(V.tensor_tensor(rank[:], ranks[:, 0, :, :], incl[:], ALU.add))
                steps.after(V.tensor_tensor(rank[:], rank[:], tot, ALU.subtract))
                steps.after(V.tensor_tensor(rank[:], rank[:], next_slot[:].unsqueeze(2).to_broadcast([P, EXPERTS, QT]),
                                            ALU.add))
                steps.after(V.tensor_tensor(rank[:], rank[:], hot[:], ALU.mult))
                steps.after(V.tensor_reduce(slot_f[:], rank[:].rearrange("p e t -> p t e"), AX_X, ALU.add))
                steps.after(V.tensor_copy(slot[:, bass.ds(b * QT, QT)], slot_f[:]))
                V.tensor_copy(batch_slot[:], slot_f[:]).then_inc(slots_ready, 1)

            def body(i, k, prepare=True):
                c, done = k % PAIRS, k >= PAIRS
                n = batch(i, k)
                if prepare:
                    scale_heads(i, k + 2)
                if c == 0 and done:
                    residual(batch(i, k, -1), n, batch(i, k, 1))
                    layer_norm_1(batch(i, k, -1), n)
                if c == 1 and done:
                    router_rows(batch(i, k, -1), n)
                if c == 3 and done:
                    choose(batch(i, k, -1), n)
                if c == 4 and k < GROUPS - LEAD:
                    x_hat(batch(i, k, 1))
                if prepare:
                    low_q(i, k + 2)
                    low_k(i, k + 2)
                normalise(i, k)
                if c == 3 and done:
                    assign(batch(i, k, -1), n)
                if c == 5 and k < GROUPS - LEAD:
                    low_xt(batch(i, k, 2))

            dve.wait_ge(x0_loaded, 16)
            x_hat(0)
            dve.wait_ge(cols_loaded, 64)
            V.tensor_scalar(scale_qk[:], gam[:], 1.0, DH ** 0.5, ALU.add, ALU.mult).then_inc(scale_ready, 1)
            low_xt(1)
            dve.wait_ge(w_split, 1)
            V.tensor_tensor(w_lo[:, 0, :], w_f[:, 0, :], w_hi[:, 0, :].bitcast(F32), ALU.subtract).then_inc(w_split, 1)
            V.memset(carry[:], 1.0).then_inc(scale_ready, 1)
            dve.wait_ge(scale_ready, 2)
            V.memset(carry[:, :, 0:1], 0.0)
            dve.wait_ge(made, 3)
            steps.after(V.tensor_copy(count[:], count_i[:]))
            V.tensor_scalar(tile_starts[:], count[:, 0:TILES], float(P), None, ALU.mult)
            V.tensor_scalar(first_slots[:], count[:, 0:EXPERTS], float(TOKENS), None, ALU.mult)
            V.tensor_scalar(next_slot[:], count[:, 0:EXPERTS], float(TOKENS), None, ALU.mult).then_inc(next_slot_ready, 1)
            dve.sem_inc(xq_free, 1)
            scale_heads(None, 0, first=True)
            low_q(None, 0)
            low_k(None, 0)
            dve.wait_ge(w_split, 3)
            V.tensor_tensor(w_lo[:, 1:PAIRS, :], w_f[:, 1:PAIRS, :], w_hi[:, 1:PAIRS, :].bitcast(F32),
                            ALU.subtract).then_inc(w_split, 1)
            scale_heads(None, 1)
            low_q(None, 1)
            low_k(None, 1)
            dve.wait_ge(x_loaded, 16)
            for k in range(LEAD):
                body(None, k)
            with dve.Fori(0, ROUNDS) as i:
                steps.restart()
                for k in range(LEAD, LEAD + PAIRS):
                    body(i, k)
            steps.restart()
            for k in range(GROUPS - LEAD, GROUPS):
                body(None, k, prepare=k + 2 < GROUPS)
            last = BATCHES - 1
            residual(last, BATCHES, BATCHES)
            layer_norm_1(last, BATCHES)
            router_rows(last, BATCHES)
            choose(last, BATCHES)
            assign(last, BATCHES)

            et = lambda a: a.rearrange("p (e t) -> p e t", e=EXPERTS)
            dve.wait_ge(next_slot_ready, BATCHES + 1)
            steps.after(V.tensor_tensor(n_tiles[:], next_slot[:], first_slots[:], ALU.subtract))
            steps.after(V.tensor_tensor(et(ra), n_tiles[:].unsqueeze(2).to_broadcast([P, EXPERTS, TILES]),
                                        tile_starts[:].unsqueeze(1).to_broadcast([P, EXPERTS, TILES]), ALU.is_gt))
            steps.after(V.tensor_reduce(n_tiles[:], et(ra), AX_X, ALU.add))
            steps.after(V.tensor_tensor_scan(ends[:], ones[:, 0:EXPERTS], n_tiles[:], 0.0, ALU.mult, ALU.add))
            all_s = [P, SLOT_TILES, EXPERTS]
            steps.after(V.tensor_tensor(cmp_s, count[:, 0:SLOT_TILES].unsqueeze(2).to_broadcast(all_s),
                                        ends[:].unsqueeze(1).to_broadcast(all_s), ALU.is_ge))
            steps.after(V.tensor_reduce(owner_f[:], cmp_s, AX_X, ALU.add))
            steps.after(V.tensor_scalar(n_tiles[:], n_tiles[:], -1.0, float(TILES), ALU.mult, ALU.add))
            steps.after(V.tensor_tensor(cmp_n, cmp_s, n_tiles[:].unsqueeze(1).to_broadcast(all_s), ALU.mult))
            steps.after(V.tensor_reduce(place_f[:], cmp_n, AX_X, ALU.add))
            steps.after(V.tensor_tensor(place[:], place_f[:], count[:, 0:SLOT_TILES], ALU.add))
            V.tensor_scalar(owner[:], owner_f[:], float(EXPERTS - 1), None, ALU.min).then_inc(owners_ready, 1)
            dve.wait_ge(owners_ready, 1)
            te7 = lambda a: a[:, 0:TILES * (EXPERTS - 1)].rearrange("p (t e) -> p t e", e=EXPERTS - 1)
            by_token = [P, TILES, EXPERTS - 1]
            steps.after(V.tensor_tensor(te7(ra), slot[:].unsqueeze(2).to_broadcast(by_token),
                                        first_slots[:, 1:EXPERTS].unsqueeze(1).to_broadcast(by_token), ALU.is_ge))
            steps.after(V.tensor_tensor(te7(rb), te7(ra), n_tiles[:, 0:EXPERTS - 1].unsqueeze(1).to_broadcast(by_token),
                                        ALU.mult))
            steps.after(V.tensor_reduce(row_f[:], te7(rb), AX_X, ALU.add))
            steps.after(V.tensor_scalar(row_f[:], row_f[:], -float(P), None, ALU.mult))
            V.tensor_tensor(row[:], row_f[:], slot[:], ALU.add).then_inc(rows_known, 1)
            dve.wait_ge(rows_known, 1)
            dve.wait_ge(ffn_loaded, 64)

            def expert(s):
                return V.value_load(owner[0:1, bass.ds(s, 1)], min_val=0, max_val=EXPERTS - 1)

            def move_xst(s, m):
                dve.wait_ge(xs_transposed, s + 1)
                V.tensor_scalar(xst[m % 3], XST, rms_col[:, 0:1], None, ALU.mult).then_inc(xst_ready, 1)

            def hidden_pre(s, m):
                e = expert(s)
                dve.wait_ge(up_done, s + 1)
                V.tensor_tensor(pre[m % 3], U[m % 3], b_1[:, bass.ds(e, 1), :].rearrange("p a b -> p (a b)"),
                                ALU.add).then_inc(pre_ready, 1)

            def hidden(s, m):
                dve.wait_ge(th_ready, s + 1)
                V.scalar_tensor_tensor(hid[m % 3], th[m % 3], 1.0, pre[m % 3], ALU.add, ALU.mult).then_inc(hid_ready, 1)

            def tile_out(s, m, stored=None):
                e = expert(s)
                dve.wait_ge(down_done, s + 1)
                if stored is not None:
                    dve.wait_ge(y_stored[m % 3], stored)
                V.tensor_tensor(ys[m % 3], Y, b_2[:, bass.ds(e, 1), :].rearrange("p a b -> p (a b)"),
                                ALU.add).then_inc(y_ready, 1)

            def tile(s, m, stored=None, up2=True, up3=True):
                if up3:
                    move_xst(s + 3, m + 3)
                if up2:
                    hidden_pre(s + 2, m + 2)
                tile_out(s, m, stored)
                if up2:
                    hidden(s + 2, m + 2)

            for s in range(3):
                move_xst(s, s)
            for s in range(2):
                hidden_pre(s, s)
                hidden(s, s)
            for s in range(3):
                tile(s, s)
            with dve.Fori(1, SLOT_TILES // 3 - 1) as i:
                for m in range(3):
                    tile(i * 3 + m, m, stored=i * 16)
            for s in range(SLOT_TILES - 3, SLOT_TILES):
                tile(s, s, stored=16 * (s // 3), up2=s + 2 < SLOT_TILES, up3=False)

            te = lambda a: a.rearrange("p (t e) -> p t e", e=EXPERTS)
            V.tensor_tensor(te(ra), logits[:], top[:].unsqueeze(2).to_broadcast([P, TILES, EXPERTS]),
                            ALU.subtract).then_inc(shifted_ready, 1)
            dve.wait_ge(score_exp_done, 1)
            steps.after(V.tensor_reduce(score[:], te(rb), AX_X, ALU.add))
            steps.after(V.reciprocal(score[:], score[:]))

            for n in range(TILES // QT):
                tiles = range(QT * n, QT * n + QT)
                dve.wait_ge(gathered[n], 16 * QT)
                for t in tiles:
                    last = V.scalar_tensor_tensor(yr[:, t, :], yr[:, t, :], score[:, t:t + 1], x[:, t, :], ALU.mult, ALU.add)
                steps.after(last)
                for m, t in enumerate(tiles):
                    last = V.bn_stats(stats[:, m, :], yr[:, t, :])
                steps.after(last)
                for m in range(QT):
                    last = V.bn_aggr(mv[:, m, :], stats[:, m, :])
                steps.after(last)
                steps.after(V.tensor_scalar(ss[:, 0:QT], mv[:, :, 1], 1.0, EPS_LN, ALU.mult, ALU.add))
                rsqrt(QT)
                for m, t in enumerate(tiles):
                    last = V.tensor_scalar(yr[:, t, :], yr[:, t, :], mv[:, m, 0:1], rs[:, m:m + 1], ALU.subtract, ALU.mult)
                last.then_inc(out_ready, 1)
                dve.wait_ge(out_ready, n + 1)

        @block.tensor
        def _(pe):
            mm = nc.tensor.matmul

            def split_mm(out_, lhs_hi, lhs_lo, rhs_hi, rhs_lo):
                mm(out_, lhs_lo, rhs_hi, start=True, stop=False)
                mm(out_, lhs_hi, rhs_lo, start=False, stop=False)
                return mm(out_, lhs_hi, rhs_hi, start=False, stop=True)

            def project(out_, t, c, a, b):
                rows = slice(t * P, (t + 1) * P)
                return split_mm(out_, xt_hi[:, rows], xt_lo[:, rows], w_hi[:, c, a:b], w_lo[:, c, a:b])

            def project_qk(i, k, b, first=False):
                pe.wait_ge(xt_ready, b)
                if not first:
                    pe.wait_ge(kt_ready, total(i, k, 1, 0))
                    pe.wait_ge(qt_ready, total(i, k, 1, 0))
                for t in range(QT):
                    last = project(ps[:, 6 + t // 2, (t % 2) * 256:(t % 2) * 256 + 256], t, k % PAIRS, 0, 2 * P)
                last.then_inc(qk_projected, 1)

            def project_v(i, k):
                pe.wait_ge(qk_scaled, total(i, k, 2, 1))
                for t in range(QT):
                    last = project(XA[:, t * P:(t + 1) * P], t, k % PAIRS, 2 * P, 3 * P)
                last.then_inc(v_projected, 1)

            def transpose_q(i, k):
                pe.wait_ge(qk_scaled, total(i, k, 2, 2))
                for t in range(QT):
                    last = nc.tensor.transpose(XB[:, t * P:(t + 1) * P], qk[:, t, 0:P], ident[:])
                last.then_inc(q_transposed, 1)

            def transpose_k(i, k):
                pe.wait_ge(v_copied, total(i, k, 1, 1))
                for t in range(QT):
                    last = nc.tensor.transpose(XA[:, t * P:(t + 1) * P], qk[:, t, P:2 * P], ident[:])
                last.then_inc(k_transposed, 1)

            def scores(i, k, j, fresh=False):
                if j == 0:
                    pe.wait_ge(qt_ready, total(i, k, 1, 1))
                    pe.wait_ge(kt_ready, total(i, k, 1, 1))
                if not fresh:
                    pe.wait_ge(tanh_done, total(i, k, 4, j - 1))
                for h in range(2):
                    rows, keys = slice(DH * h, DH * (h + 1)), slice(j * P, (j + 1) * P)
                    last = split_mm(S[j % 2][:, h, :], kt_hi[rows, k % 2, keys], kt_lo[rows, k % 2, keys],
                                    qt_hi[rows, k % 2, :], qt_lo[rows, k % 2, :])
                last.then_inc(scored, 1)

            def pv(i, k, j, first=False):
                if j % 2 == 0:
                    pe.wait_ge(exp_done, total(i, k, 2, j // 2 + 1))
                if j == 0:
                    pe.wait_ge(v_copied, total(i, k, 1, 1))
                    if not first:
                        pe.wait_ge(at_ready, total(i, k, 1, 0))
                for h in range(2):
                    last = mm(AV[DH * h:DH * (h + 1), :], v[:, k % 4, j, DH * h:DH * (h + 1)],
                              pr[:, k % 2, j, h * SEQ:(h + 1) * SEQ], start=j == 0, stop=j == QT - 1)
                if j == QT - 1:
                    last.then_inc(pv_done, 1)

            def softmax_sums(i, k):
                pe.wait_ge(sums_ready, total(i, k, 1, 1))
                for h in range(2):
                    last = mm(DEN[DH * h:DH * (h + 1), :], ones[:, 0:DH], sums[:, h * SEQ:(h + 1) * SEQ],
                              start=True, stop=True)
                last.then_inc(den_done, 1)

            def output_projection(n):
                for t in range(QT):
                    for c in range(PAIRS):
                        last = mm(DEN[:, t * D:(t + 1) * D], at[:, c, t * P:(t + 1) * P], w_o[:, c, :],
                                  start=c == 0, stop=c == PAIRS - 1)
                last.then_inc(wo_done, 1)

            def transpose_rows(rows, done):
                for t in range(QT):
                    last = nc.tensor.transpose(XB[:, t * P:(t + 1) * P], rows[:, t, :], ident[:])
                last.then_inc(done, 1)

            def router_logits(n):
                pe.wait_ge(xrt_ready, n)
                for t in range(QT):
                    last = mm(XB[:, t * EXPERTS:(t + 1) * EXPERTS], xrt[:, t * P:(t + 1) * P], gate_t[:],
                              start=True, stop=True)
                last.then_inc(logits_done, 1)

            def rank_tokens(n):
                pe.wait_ge(hot_ready, n)
                w, hots = QT * EXPERTS, hot[:].rearrange("p e t -> p (e t)")
                mm(XB[:, 0:w], before[:], hots, start=True, stop=True)
                mm(XB[:, w:2 * w], ones[:], hots, start=True, stop=True).then_inc(ranked, 1)

            def body(i, k, first=False):
                c, done = k % PAIRS, k >= PAIRS
                prepare, score_next = k + 2 < GROUPS, k + 1 < GROUPS
                n = batch(i, k)
                for j in range(QT):
                    if score_next:
                        scores(i, k + 1, j)
                    if j == 0 and prepare:
                        if c == 2 and done:
                            pe.wait_ge(xrt_ready, n)
                        if c == 3 and done:
                            pe.wait_ge(logits_copied, n)
                        project_qk(i, k + 2, batch(i, k + 2, 1))
                    if j == 3 and prepare:
                        transpose_q(i, k + 2)
                        transpose_k(i, k + 2)
                    pv(i, k, j, first)
                    if j == 0 and c == 0 and done:
                        output_projection(n)
                    if j == 2 and prepare:
                        project_v(i, k + 2)
                if c == 0 and done:
                    pe.wait_ge(x1_ready, n)
                softmax_sums(i, k)
                if c in (1, 2, 3) and done or c == 5 and k < GROUPS - LEAD:
                    if prepare:
                        pe.wait_ge(qt_ready, total(i, k + 2, 1, 1))
                    if c == 1:
                        pe.wait_ge(xq_ready, n)
                        transpose_rows(xq, xq_transposed)
                    if c == 2:
                        router_logits(n)
                    if c == 3:
                        rank_tokens(n)
                        pe.wait_ge(ranks_copied, n)
                    if c == 5:
                        pe.wait_ge(xh_ready, batch(i, k, 2))
                        transpose_rows(xh, xt_transposed)

            pe.wait_ge(consts_ready, 2)
            pe.wait_ge(xh_ready, 1)
            transpose_rows(xh, xt_transposed)
            pe.wait_ge(w_split, 2)
            project_qk(None, 0, 1, first=True)
            project_v(None, 0)
            transpose_q(None, 0)
            transpose_k(None, 0)
            pe.wait_ge(w_split, 4)
            project_qk(None, 1, 1)
            scores(None, 0, 0, fresh=True)
            scores(None, 0, 1, fresh=True)
            project_v(None, 1)
            scores(None, 0, 2)
            transpose_q(None, 1)
            scores(None, 0, 3)
            transpose_k(None, 1)
            pe.wait_ge(wo_loaded, 32)
            for k in range(LEAD):
                body(None, k, first=k == 0)
            with pe.Fori(0, ROUNDS) as i:
                for k in range(LEAD, LEAD + PAIRS):
                    body(i, k)
            for k in range(GROUPS - LEAD, GROUPS):
                body(None, k)

            pe.wait_ge(at_ready, GROUPS)
            output_projection(BATCHES)
            pe.wait_ge(xq_ready, BATCHES)
            transpose_rows(xq, xq_transposed)
            router_logits(BATCHES)
            rank_tokens(BATCHES)

            def expert(s):
                return nc.tensor.value_load(owner[0:1, bass.ds(s, 1)], min_val=0, max_val=EXPERTS - 1)

            def transpose_x(m, loaded):
                pe.wait_ge(xs_loaded[m % 3], loaded)
                nc.tensor.transpose(XST, xs[m % 3], ident[:]).then_inc(xs_transposed, 1)

            def up(s, m, fresh=False):
                e = expert(s)
                pe.wait_ge(xst_ready, s + 1)
                if not fresh:
                    pe.wait_ge(pre_ready, s - 2)
                mm(U[m % 3], xst[m % 3], w_1[:, bass.ds(e, 1), :].rearrange("p a b -> p (a b)"),
                   start=True, stop=True).then_inc(up_done, 1)

            def tile(s, m, loaded=None, first=False, ahead2=True):
                pe.wait_ge(hid_ready, s + 1)
                if not first:
                    pe.wait_ge(ht_copied, s)
                for f in range(FK):
                    last = nc.tensor.transpose(HT[:, f * P:(f + 1) * P], hid[m % 3][:, f * P:(f + 1) * P], ident[:])
                last.then_inc(h_transposed, 1)
                if ahead2:
                    up(s + 2, m + 2, fresh=first)
                if loaded is not None:
                    pe.wait_ge(xst_ready, s + 3)
                    transpose_x(m + 3, loaded)
                e = expert(s)
                pe.wait_ge(ht_copied, s + 1)
                if not first:
                    pe.wait_ge(y_ready, s)
                for f in range(FK):
                    last = mm(Y, ht_sb[:, f * P:(f + 1) * P],
                              w_2[:, bass.ds(e, 1), f * D:(f + 1) * D].rearrange("p a b -> p (a b)"),
                              start=f == 0, stop=f == FK - 1)
                last.then_inc(down_done, 1)

            pe.wait_ge(owners_ready, 1)
            pe.wait_ge(ffn_loaded, 64)
            for s in range(3):
                if s:
                    pe.wait_ge(xst_ready, s)
                transpose_x(s, 16)
            up(0, 0, fresh=True)
            up(1, 1, fresh=True)
            for s in range(3):
                tile(s, s, loaded=32, first=s == 0)
            with pe.Fori(1, SLOT_TILES // 3 - 1) as i:
                for m in range(3):
                    tile(i * 3 + m, m, loaded=i * 16 + 32)
            for s in range(SLOT_TILES - 3, SLOT_TILES):
                tile(s, s, ahead2=s + 2 < SLOT_TILES)


_ORDER = ["tokens", "norm_w", "wq", "wkv", "wo", "q_gamma", "k_gamma", "rms_w", "gate_w", "w1", "b1", "w2", "b2"]


def kernel(L0_attn_tokens, L0_attn_norm_w, L0_attn_Wq, L0_attn_Wkv, L0_attn_Wo, L0_attn_q_gamma,
           L0_attn_k_gamma, L0_ffn_rms_w, L0_ffn_gate_w, L0_ffn_W1, L0_ffn_b1, L0_ffn_W2, L0_ffn_b2):
    import numpy as np
    import concourse.bacc as bacc
    from concourse.bass_utils import run_bass_kernel_spmd

    def column(a):
        return np.ascontiguousarray(np.asarray(a).reshape(-1, P).T)

    arrays = dict(
        tokens=np.asarray(L0_attn_tokens).reshape(TOKENS, D),
        norm_w=column(L0_attn_norm_w), wq=np.asarray(L0_attn_Wq), wkv=np.asarray(L0_attn_Wkv),
        wo=np.asarray(L0_attn_Wo), q_gamma=column(L0_attn_q_gamma), k_gamma=column(L0_attn_k_gamma),
        rms_w=column(L0_ffn_rms_w), gate_w=np.ascontiguousarray(np.asarray(L0_ffn_gate_w).T),
        w1=np.asarray(L0_ffn_W1), b1=np.asarray(L0_ffn_b1).reshape(1, -1),
        w2=np.asarray(L0_ffn_W2), b2=np.asarray(L0_ffn_b2).reshape(1, -1),
    )
    nc = bacc.Bacc("TRN2", target_bir_lowering=False, num_devices=1)
    args = [nc.dram_tensor(f"in_{n}", arrays[n].shape, F32, kind="ExternalInput").ap() for n in _ORDER]
    out = nc.dram_tensor("out", [TOKENS, D], F32, kind="ExternalOutput").ap()
    build(nc, *args, out)
    r = run_bass_kernel_spmd(nc, [{f"in_{n}": np.ascontiguousarray(arrays[n]) for n in _ORDER}], core_ids=[0])
    return r.results[0]["out"].reshape(BATCHES, SEQ, D)
```

```python
from contextlib import ExitStack

import concourse.bass as bass
import concourse.mybir as mybir

F32 = mybir.dt.float32
F32R = mybir.dt.float32r
I32 = mybir.dt.int32
ALU = mybir.AluOpType
ACT = mybir.ActivationFunctionType
AX_X = mybir.AxisListType.X

P = 128
D = 128
HEADS, DH = 16, 64
BATCHES, SEQ = 8, 512
TOKENS = BATCHES * SEQ
PAIRS = HEADS // 2
GROUPS = BATCHES * PAIRS
QT = SEQ // P
TILES = TOKENS // P
EXPERTS, FF = 8, 512
FK = FF // P
SLOT_TILES = TILES + EXPERTS - 1
DRAM_TILES = EXPERTS * TILES + EXPERTS - 1
ZERO_TILES = 32
ZEROS_STORED = 16 * -(-DRAM_TILES // ZERO_TILES)
CLAMP = 50.0
EPS_ATTN = 1.1920928955078125e-07
EPS_FFN = 1e-6
EPS_LN = 1e-5
TINY = 1e-24
RSQRT_MAGIC = float(0x5F3759DF)


class Steps:

    def __init__(self, engine, sem):
        self.engine, self.sem, self.n = engine, sem, 0

    def restart(self):
        self.engine.sem_clear(self.sem)
        self.n = 0

    def after(self, instruction):
        instruction.then_inc(self.sem, 1)
        self.n += 1
        self.engine.wait_ge(self.sem, self.n)


def build(nc, tokens, norm_w, wq, wkv, wo, q_gamma, k_gamma, rms_w, gate_w, w1, b1, w2, b2, out):
    sorted_x = nc.dram_tensor("sorted_x", [DRAM_TILES * P, D], F32, kind="Internal").ap()
    sorted_y = nc.dram_tensor("sorted_y", [SLOT_TILES * P, D], F32, kind="Internal").ap()

    with ExitStack() as ctx:
        def sb(name, shape, dt=F32):
            return ctx.enter_context(nc.sbuf_tensor(name, shape, dt))

        def sem(name):
            return ctx.enter_context(nc.semaphore(name))

        w_hi = sb("w_hi", [P, PAIRS, 3 * P], F32R)
        w_lo = sb("w_lo", [P, PAIRS, 3 * P], F32R)
        w_o = sb("w_o", [P, PAIRS, D])
        w_1 = sb("w_1", [P, EXPERTS, FF])
        w_2 = sb("w_2", [P, EXPERTS, FK * D])
        b_1 = sb("b_1", [P, EXPERTS, FF])
        b_2 = sb("b_2", [P, EXPERTS, D])
        gate_t = sb("gate_t", [P, EXPERTS])
        norm_col = sb("norm_col", [P, 1])
        rms_col = sb("rms_col", [P, 1])
        gam = sb("gam", [P, 2, PAIRS])
        scale_qk = sb("scale_qk", [P, 2, PAIRS])
        ident = sb("ident", [P, P])
        ones = sb("ones", [P, P])
        before = sb("before", [P, P])
        count_i = sb("count_i", [P, 64], I32)
        count = sb("count", [P, 64])
        tile_starts = sb("tile_starts", [P, TILES])
        first_slots = sb("first_slots", [P, EXPERTS])
        carry = sb("carry", [P, EXPERTS, QT])
        zeros = b_1[:].rearrange("p e f -> p (e f)")

        x = sb("x", [P, TILES, D])
        xh = sb("xh", [P, QT, D])
        xq = sb("xq", [P, QT, D])
        xt_hi = sb("xt_hi", [P, SEQ], F32R)
        xt_lo = sb("xt_lo", [P, SEQ], F32R)
        sq = sb("sq", [P, 4, 2 * P])
        qk = sb("qk", [P, QT, 2 * P])
        qt_hi = sb("qt_hi", [P, 2, SEQ], F32R)
        qt_lo = sb("qt_lo", [P, 2, SEQ], F32R)
        kt_hi = sb("kt_hi", [P, 2, SEQ], F32R)
        kt_lo = sb("kt_lo", [P, 2, SEQ], F32R)
        v = sb("v", [P, 4, QT, P])
        pr = sb("pr", [P, 2, QT, 2 * SEQ])
        part = sb("part", [P, 2, 2 * SEQ])
        sums = sb("sums", [P, 2 * SEQ])
        den_t = sb("den_t", [P, SEQ])
        den_r = sb("den_r", [P, SEQ // 32])
        at = sb("at", [P, PAIRS, SEQ])
        xrt = sb("xrt", [P, SEQ])
        ss = sb("ss", [P, 64])
        rs = sb("rs", [P, 64])
        na = sb("na", [P, 64])
        stats = sb("stats", [P, QT, 6])
        mv = sb("mv", [P, QT, 2])
        nb = sb("nb", [P, 64])

        logits = sb("logits", [P, TILES, EXPERTS])
        top = sb("top", [P, TILES])
        is_top = sb("is_top", [P, QT, EXPERTS])
        choice = sb("choice", [P, QT, EXPERTS])
        least = sb("least", [P, QT])
        hot = sb("hot", [P, EXPERTS, QT])
        batch_logits = sb("batch_logits", [P, QT, EXPERTS])
        ranks = sb("ranks", [P, 2, EXPERTS, QT])
        tot = ranks[:, 1, :, :]
        incl = sb("incl", [P, EXPERTS, QT])
        rank = sb("rank", [P, EXPERTS, QT])
        slot_f = sb("slot_f", [P, QT])
        batch_slot = sb("batch_slot", [P, QT], I32)
        next_slot = sb("next_slot", [P, EXPERTS])
        slot = sb("slot", [P, TILES], I32)
        score = sb("score", [P, TILES])
        row_f = sb("row_f", [P, TILES])
        row = sb("row", [P, TILES], I32)
        n_tiles = sb("n_tiles", [P, EXPERTS])
        ends = sb("ends", [P, EXPERTS])
        owner_f = sb("owner_f", [P, SLOT_TILES])
        owner = sb("owner", [P, SLOT_TILES], I32)
        place_f = sb("place_f", [P, SLOT_TILES])
        place = sb("place", [P, SLOT_TILES], I32)
        ra, rb = at[:, 0, 0:TILES * EXPERTS], at[:, 0, TILES * EXPERTS:2 * TILES * EXPERTS]
        cmp_s = at[:, 4, 0:SLOT_TILES * EXPERTS].rearrange("p (s e) -> p s e", e=EXPERTS)
        cmp_n = at[:, 5, 0:SLOT_TILES * EXPERTS].rearrange("p (s e) -> p s e", e=EXPERTS)

        w_f = pr[:, 1, :, :].rearrange("p a b -> p (a b)")[:, 0:PAIRS * 3 * P].rearrange("p (c n) -> p c n", c=PAIRS)

        p0 = pr[:, 0, :, :].rearrange("p a b -> p (a b)")
        p1 = pr[:, 1, :, :].rearrange("p a b -> p (a b)")
        pre = [p0[:, m * FF:(m + 1) * FF] for m in range(3)]
        th = [p0[:, (3 + m) * FF:(4 + m) * FF] for m in range(3)]
        ht_sb = p0[:, 6 * FF:7 * FF]
        hid = [p1[:, m * FF:(m + 1) * FF] for m in range(3)]
        xs = [p1[:, 3 * FF + m * P:3 * FF + (m + 1) * P] for m in range(3)]
        xst = [p1[:, 3 * FF + (3 + m) * P:3 * FF + (4 + m) * P] for m in range(3)]
        ys = [p1[:, 3 * FF + (6 + m) * P:3 * FF + (7 + m) * P] for m in range(3)]
        yr = pr[:].rearrange("p a b c -> p (a b c)")[:, 0:TILES * D].rearrange("p (t d) -> p t d", d=D)

        ps = ctx.enter_context(nc.psum_tensor("ps", [P, 8, 512], F32))
        S = [ps[:, 2 * k:2 * k + 2, :] for k in range(2)]
        AV, DEN, XA, XB = ps[:, 4, :], ps[:, 5, :], ps[:, 6, :], ps[:, 7, :]
        U = [ps[:, m, :] for m in range(3)]
        HT, Y, XST = ps[:, 3, :], ps[:, 4, 0:D], ps[:, 5, 0:P]

        x0_loaded, x_loaded = sem("x0_loaded"), sem("x_loaded")
        w_first_loaded, w_loaded, cols_loaded = sem("w_first_loaded"), sem("w_loaded"), sem("cols_loaded")
        wo_loaded, ffn_loaded = sem("wo_loaded"), sem("ffn_loaded")
        w_split = sem("w_split")
        zeroed = sem("zeroed")
        zeros_stored = sem("zeros_stored")
        made, consts_ready, scale_ready = sem("made"), sem("consts_ready"), sem("scale_ready")
        dve_steps, pool_steps = sem("dve_steps"), sem("pool_steps")
        xh_ready, xt_transposed = sem("xh_ready"), sem("xt_transposed")
        xt_hi_ready, xt_ready = sem("xt_hi_ready"), sem("xt_ready")
        qk_projected = sem("qk_projected")
        squared, qk_scaled = sem("squared"), sem("qk_scaled")
        squares_summed = sem("squares_summed")
        v_projected, v_copied = sem("v_projected"), sem("v_copied")
        q_transposed, qt_hi_ready, qt_ready = sem("q_transposed"), sem("qt_hi_ready"), sem("qt_ready")
        k_transposed, kt_hi_ready, kt_ready = sem("k_transposed"), sem("kt_hi_ready"), sem("kt_ready")
        scored, tanh_done, exp_done = sem("scored"), sem("tanh_done"), sem("exp_done")
        pv_done, sums_ready, den_done, at_ready = sem("pv_done"), sem("sums_ready"), sem("den_done"), sem("at_ready")
        wo_done, x1_ready = sem("wo_done"), sem("x1_ready")
        xq_ready, xq_transposed, xrt_ready = sem("xq_ready"), sem("xq_transposed"), sem("xrt_ready")
        logits_done, logits_copied = sem("logits_done"), sem("logits_copied")
        hot_ready, ranked, ranks_copied = sem("hot_ready"), sem("ranked"), sem("ranks_copied")
        slots_ready = sem("slots_ready")
        next_slot_ready, xq_free = sem("next_slot_ready"), sem("xq_free")
        scattered = sem("scattered")
        rows_known = sem("rows_known")
        owners_ready, shifted_ready, score_exp_done = sem("owners_ready"), sem("shifted_ready"), sem("score_exp_done")
        xs_loaded = [sem(f"xs_loaded{m}") for m in range(3)]
        y_stored = [sem(f"y_stored{m}") for m in range(3)]
        xs_transposed, xst_ready, up_done = sem("xs_transposed"), sem("xst_ready"), sem("up_done")
        pre_ready, th_ready, hid_ready = sem("pre_ready"), sem("th_ready"), sem("hid_ready")
        h_transposed, ht_copied, down_done, y_ready = sem("h_transposed"), sem("ht_copied"), sem("down_done"), sem("y_ready")
        gathered = [sem(f"gathered{n}") for n in range(TILES // QT)]
        out_ready, out_stored = sem("out_ready"), sem("out_stored")

        block = ctx.enter_context(nc.Block())

        LEAD = 4
        ROUNDS = BATCHES - 1

        def total(i, k, each, plus):
            n = each * k + plus
            return n if i is None else i * (each * PAIRS) + n

        def batch(i, k, plus=0):
            n = k // PAIRS + plus
            return n if i is None else i + n

        @block.sync
        def _(sp):
            xv = tokens.rearrange("(t p) d -> p t d", p=P)
            sp.dma_start(x[:, 0:QT, :], xv[:, 0:QT, :]).then_inc(x0_loaded, 16)
            for n, w in enumerate((wq, wkv[:, 0:HEADS * DH], wkv[:, HEADS * DH:2 * HEADS * DH])):
                sp.dma_start(w_f[:, 0, n * P:(n + 1) * P], w[:, 0:P]).then_inc(w_first_loaded, 16)
            sp.dma_start(norm_col[:], norm_w).then_inc(cols_loaded, 16)
            sp.dma_start(gam[:, 0, :], q_gamma).then_inc(cols_loaded, 16)
            sp.dma_start(gam[:, 1, :], k_gamma).then_inc(cols_loaded, 16)
            sp.dma_start(rms_col[:], rms_w).then_inc(cols_loaded, 16)
            for n, w in enumerate((wq, wkv[:, 0:HEADS * DH], wkv[:, HEADS * DH:2 * HEADS * DH])):
                sp.dma_start(w_f[:, 1:PAIRS, n * P:(n + 1) * P],
                             w[:, P:PAIRS * P].rearrange("d (c n) -> d c n", n=P)).then_inc(w_loaded, 16)
            sp.dma_start(x[:, QT:TILES, :], xv[:, QT:TILES, :]).then_inc(x_loaded, 16)
            sp.dma_start(w_o[:], wo.rearrange("(c p) n -> p c n", p=P)).then_inc(wo_loaded, 16)
            sp.dma_start(gate_t[:], gate_w).then_inc(wo_loaded, 16)
            sp.wait_ge(zeroed, 1)
            zv = sorted_x.rearrange("(p t) d -> p (t d)", p=P)
            for t in range(0, DRAM_TILES, ZERO_TILES):
                n = min(ZERO_TILES, DRAM_TILES - t) * D
                sp.dma_start(zv[:, t * D:t * D + n], zeros[:, 0:n]).then_inc(zeros_stored, 16)
            sp.dma_start(w_1[:], w1.rearrange("e d f -> d e f")).then_inc(ffn_loaded, 16)
            sp.dma_start(w_2[:].rearrange("p e (k n) -> p (e k) n", k=FK),
                         w2.rearrange("e (k p) n -> p (e k) n", p=P)).then_inc(ffn_loaded, 16)
            sp.wait_ge(zeros_stored, ZEROS_STORED)
            sp.dma_start(b_1[:].rearrange("p e f -> p (e f)"), b1.to_broadcast([P, EXPERTS * FF])).then_inc(ffn_loaded, 16)
            sp.dma_start(b_2[:].rearrange("p e f -> p (e f)"), b2.to_broadcast([P, EXPERTS * D])).then_inc(ffn_loaded, 16)

            def load(s, m):
                t = sp.value_load(place[0:1, bass.ds(s, 1)], min_val=0, max_val=DRAM_TILES - 1)
                sp.dma_start(xs[m % 3], sorted_x[bass.ds(t * P, P), :]).then_inc(xs_loaded[m % 3], 16)

            sp.wait_ge(owners_ready, 1)
            sp.wait_ge(scattered, 16 * TILES)
            for m in range(3):
                load(m, m)
            with sp.Fori(1, SLOT_TILES // 3) as i:
                for m in range(3):
                    sp.wait_ge(xs_transposed, i * 3 + m - 2)
                    load(i * 3 + m, m)
            ov = out.rearrange("(t p) d -> p t d", p=P)
            for n in range(TILES // QT):
                sp.wait_ge(out_ready, n + 1)
                sp.dma_start(ov[:, QT * n:QT * (n + 1), :], yr[:, QT * n:QT * (n + 1), :]).then_inc(out_stored, 16)
            sp.wait_ge(out_stored, 16 * (TILES // QT))

        @block.gpsimd
        def _(pool):
            steps = Steps(pool, pool_steps)
            nc.gpsimd.memset(ident[:], 0.0).then_inc(made, 1)
            nc.gpsimd.memset(ones[:], 1.0).then_inc(made, 1)
            nc.gpsimd.iota(count_i[:], pattern=[[1, 64]], base=0, channel_multiplier=0).then_inc(made, 1)
            pool.wait_ge(made, 3)
            nc.gpsimd.affine_select(out=ident[:], in_=ident[:], compare_op=ALU.not_equal, fill=1.0, base=0,
                                    pattern=[[-1, P]], channel_multiplier=1).then_inc(consts_ready, 1)
            nc.gpsimd.affine_select(out=before[:], in_=ones[:], compare_op=ALU.is_gt, fill=0.0, base=0,
                                    pattern=[[1, P]], channel_multiplier=-1).then_inc(consts_ready, 1)
            nc.gpsimd.memset(zeros, 0.0).then_inc(zeroed, 1)

            def body(i, k, first=False):
                pair = pr[:, k % 2, :, :]
                pool.wait_ge(exp_done, total(i, k, 2, 1))
                steps.after(nc.gpsimd.tensor_tensor(part[:, 0, :], pair[:, 0, :], pair[:, 1, :], ALU.add))
                pool.wait_ge(exp_done, total(i, k, 2, 2))
                steps.after(nc.gpsimd.tensor_tensor(part[:, 1, :], pair[:, 2, :], pair[:, 3, :], ALU.add))
                if not first:
                    pool.wait_ge(den_done, total(i, k, 1, 0))
                nc.gpsimd.tensor_tensor(sums[:], part[:, 0, :], part[:, 1, :], ALU.add).then_inc(sums_ready, 1)
                if k % PAIRS == 3 and k > PAIRS:
                    scatter(batch(i, k))
                pool.wait_ge(sums_ready, total(i, k, 1, 1))

            def scatter(n):
                pool.wait_ge(slots_ready, n)
                nc.gpsimd.tensor_tensor(next_slot[:], next_slot[:], incl[:, :, QT - 1], ALU.add).then_inc(next_slot_ready, 1)
                pool.wait_ge(zeros_stored, ZEROS_STORED)
                for t in range(QT):
                    nc.gpsimd.indirect_dma_start(
                        out=sorted_x, out_offset=bass.IndirectOffsetOnAxis(ap=batch_slot[:, t:t + 1], axis=0),
                        in_=xq[:, t, :], in_offset=None).then_inc(scattered, 16)
                pool.wait_ge(scattered, n * (16 * QT))
                pool.sem_inc(xq_free, 1)

            for k in range(LEAD):
                body(None, k, first=k == 0)
            with pool.Fori(0, ROUNDS) as i:
                steps.restart()
                for k in range(LEAD, LEAD + PAIRS):
                    body(i, k)
            steps.restart()
            for k in range(GROUPS - LEAD, GROUPS):
                body(None, k)
            scatter(BATCHES)
            for m in range(3):
                pool.wait_ge(y_stored[m], 16 * (SLOT_TILES // 3))
            pool.wait_ge(rows_known, 1)
            for t in range(TILES):
                nc.gpsimd.indirect_dma_start(
                    out=yr[:, t, :], out_offset=None, in_=sorted_y,
                    in_offset=bass.IndirectOffsetOnAxis(ap=row[:, t:t + 1], axis=0)).then_inc(gathered[t // QT], 16)

        @block.scalar
        def _(act):
            def squares(i, k, first=False):
                act.wait_ge(qk_projected, total(i, k, 1, 1))
                if not first:
                    act.wait_ge(squares_summed, total(i, k, 1, 0))
                nc.scalar.activation(sq[:].rearrange("p a b -> p (a b)"),
                                     ps[:, 6:8, :].rearrange("p a b -> p (a b)"), ACT.Square).then_inc(squared, 1)

            def copy_v(g, half, copies):
                act.wait_ge(v_projected, copies)
                nc.scalar.activation(v[:, g % 4:g % 4 + 2, 2 * half:2 * half + 2, :].rearrange("p g t d -> p t g d"),
                                     DEN.rearrange("p (t g d) -> p t g d", t=2, g=2), ACT.Copy).then_inc(v_copied, 1)

            def tanh(i, k, j):
                act.wait_ge(scored, total(i, k, 4, j + 1))
                nc.scalar.activation(pr[:, k % 2, j, :], S[j % 2].rearrange("p a b -> p (a b)"), ACT.Tanh,
                                     scale=1.0 / CLAMP).then_inc(tanh_done, 1)

            def exps(i, k, half):
                act.wait_ge(tanh_done, total(i, k, 4, 2 * half + 2))
                w = pr[:, k % 2, 2 * half:2 * half + 2, :].rearrange("p a b -> p (a b)")
                nc.scalar.activation(w, w, ACT.Exp, scale=CLAMP / DH ** 0.5).then_inc(exp_done, 1)

            def high(dst, src, scale, done):
                nc.scalar.activation(dst, src, ACT.Copy, scale=scale).then_inc(done, 1)

            def high_q(i, k):
                act.wait_ge(q_transposed, total(i, k, 1, 1))
                high(qt_hi[:, k % 2, :], XB, scale_qk[:, 0, k % PAIRS:k % PAIRS + 1], qt_hi_ready)

            def high_k(i, k):
                act.wait_ge(k_transposed, total(i, k, 1, 1))
                high(kt_hi[:, k % 2, :], XA, scale_qk[:, 1, k % PAIRS:k % PAIRS + 1], kt_hi_ready)

            def high_xt(n):
                act.wait_ge(xt_transposed, n)
                high(xt_hi[:], DEN, norm_col[:, 0:1], xt_hi_ready)

            def router_steps(c, n):
                if c == 1:
                    act.wait_ge(xq_transposed, n)
                    high(xrt[:], DEN, rms_col[:, 0:1], xrt_ready)
                if c == 2:
                    act.wait_ge(logits_done, n)
                    high(batch_logits[:].rearrange("p a b -> p (a b)"), DEN[:, 0:QT * EXPERTS], 1.0, logits_copied)
                if c == 3:
                    act.wait_ge(ranked, n)
                    high(ranks[:].rearrange("p a e t -> p (a e t)"), DEN[:, 0:2 * QT * EXPERTS], 1.0, ranks_copied)

            def body(i, k, first=False, prepare=True, score_next=True):
                c, done = k % PAIRS, k >= PAIRS
                if score_next:
                    if not first:
                        act.wait_ge(pv_done, total(i, k, 1, 0))
                        act.wait_ge(sums_ready, total(i, k, 1, 0))
                    tanh(i, k + 1, 0)
                if prepare:
                    squares(i, k + 2)
                if score_next:
                    tanh(i, k + 1, 1)
                if done and c in (2, 3):
                    router_steps(c, batch(i, k))
                if score_next:
                    exps(i, k + 1, 0)
                    tanh(i, k + 1, 2)
                if prepare:
                    copy_v(k + 2 - k % 2, k % 2, total(i, k, 1, 3))
                    high_q(i, k + 2)
                    high_k(i, k + 2)
                if score_next:
                    tanh(i, k + 1, 3)
                if done and c == 1:
                    router_steps(c, batch(i, k))
                if c == 5 and k < GROUPS - LEAD:
                    high_xt(batch(i, k, 2))
                if score_next:
                    exps(i, k + 1, 1)

            act.wait_ge(cols_loaded, 64)
            high_xt(1)
            act.wait_ge(w_first_loaded, 48)
            high(w_hi[:, 0, :], w_f[:, 0, :], 1.0, w_split)
            act.wait_ge(scale_ready, 1)
            squares(None, 0, first=True)
            high_q(None, 0)
            high_k(None, 0)
            act.wait_ge(w_loaded, 48)
            high(w_hi[:, 1:PAIRS, :], w_f[:, 1:PAIRS, :], 1.0, w_split)
            squares(None, 1)
            tanh(None, 0, 0)
            tanh(None, 0, 1)
            exps(None, 0, 0)
            copy_v(0, 0, 1)
            tanh(None, 0, 2)
            high_q(None, 1)
            high_k(None, 1)
            copy_v(0, 1, 2)
            tanh(None, 0, 3)
            exps(None, 0, 1)
            act.wait_ge(w_split, 4)
            for k in range(LEAD):
                body(None, k, first=k == 0)
            with act.Fori(0, ROUNDS) as i:
                for k in range(LEAD, LEAD + PAIRS):
                    body(i, k)
            for k in range(GROUPS - LEAD, GROUPS):
                body(None, k, prepare=k + 2 < GROUPS, score_next=k + 1 < GROUPS)

            for c in (1, 2, 3):
                router_steps(c, BATCHES)

            def tanh_pre(s, m):
                act.wait_ge(pre_ready, s + 1)
                nc.scalar.activation(th[m % 3], pre[m % 3], ACT.Tanh, scale=0.5).then_inc(th_ready, 1)

            def store(s, m):
                act.wait_ge(y_ready, s + 1)
                act.dma_start(sorted_y[bass.ds(s * P, P), :], ys[m % 3]).then_inc(y_stored[m % 3], 16)

            def tile(s, m, first=False, ahead=True):
                act.wait_ge(h_transposed, s + 1)
                if not first:
                    act.wait_ge(down_done, s)
                nc.scalar.activation(ht_sb, HT, ACT.Copy, scale=0.5).then_inc(ht_copied, 1)
                if ahead:
                    tanh_pre(s + 2, m + 2)
                if not first:
                    store(s - 1, m + 2)

            act.wait_ge(owners_ready, 1)
            tanh_pre(0, 0)
            tanh_pre(1, 1)
            for s in range(3):
                tile(s, s, first=s == 0)
            with act.Fori(1, SLOT_TILES // 3 - 1) as i:
                for m in range(3):
                    tile(i * 3 + m, m)
            for s in range(SLOT_TILES - 3, SLOT_TILES):
                tile(s, s, ahead=s + 2 < SLOT_TILES)
            store(SLOT_TILES - 1, SLOT_TILES - 1)

            act.wait_ge(shifted_ready, 1)
            nc.scalar.activation(rb, ra, ACT.Exp).then_inc(score_exp_done, 1)

        @block.vector
        def _(dve):
            V = nc.vector
            steps = Steps(dve, dve_steps)

            def rsqrt(cols):
                y, s, a, b = rs[:, cols], ss[:, cols], na[:, cols], nb[:, cols]
                steps.after(V.tensor_scalar(y.bitcast(I32), s.bitcast(I32), -0.5, RSQRT_MAGIC, ALU.mult, ALU.add))
                steps.after(V.tensor_tensor(a, y, s, ALU.mult))
                steps.after(V.tensor_tensor(b, a, y, ALU.mult))
                steps.after(V.scalar_tensor_tensor(a, b, -10.0 / 3.0, b, ALU.add, ALU.mult))
                steps.after(V.scalar_tensor_tensor(y, a, 5.0, y, ALU.add, ALU.mult))
                steps.after(V.scalar_tensor_tensor(a, y, -0.5 * 0.375 ** 3, s, ALU.mult, ALU.mult))
                steps.after(V.tensor_tensor(b, a, y, ALU.mult))
                steps.after(V.scalar_tensor_tensor(y, b, 1.5 * 0.375, y, ALU.add, ALU.mult))

            HEAD_COLS = slice(0, 16)
            ROW_COLS = slice(16, 16 + QT)

            def rows_squares(rows, eps):
                tmp = den_t[:].rearrange("p (a b) -> p a b", b=D)
                steps.after(V.tensor_tensor(tmp, rows, rows, ALU.mult))
                steps.after(V.tensor_reduce(ss[:, ROW_COLS], tmp, AX_X, ALU.add))
                steps.after(V.tensor_scalar(ss[:, ROW_COLS], ss[:, ROW_COLS], 1.0 / D, eps, ALU.mult, ALU.add))

            def centre(rows, tmp):
                steps.after(V.tensor_reduce(ss[:, ROW_COLS], rows, AX_X, ALU.add))
                steps.after(V.tensor_scalar(ss[:, ROW_COLS], ss[:, ROW_COLS], 1.0 / D, None, ALU.mult))
                steps.after(V.tensor_tensor(rows, rows, ss[:, ROW_COLS].unsqueeze(2).to_broadcast([P, QT, D]), ALU.subtract))
                steps.after(V.tensor_tensor(tmp, rows, rows, ALU.mult))
                steps.after(V.tensor_reduce(ss[:, ROW_COLS], tmp, AX_X, ALU.add))
                steps.after(V.tensor_scalar(ss[:, ROW_COLS], ss[:, ROW_COLS], 1.0 / D, EPS_LN, ALU.mult, ALU.add))
                rsqrt(ROW_COLS)

            def scale_heads(i, k, first=False):
                dve.wait_ge(squared, total(i, k, 1, 1))
                V.tensor_reduce(ss[:, HEAD_COLS], sq[:].rearrange("p a (h d) -> p (a h) d", d=DH), AX_X,
                                ALU.add).then_inc(squares_summed, 1)
                dve.wait_ge(squares_summed, total(i, k, 1, 1))
                steps.after(V.tensor_scalar(ss[:, HEAD_COLS], ss[:, HEAD_COLS], TINY, None, ALU.max))
                rsqrt(HEAD_COLS)
                if not first:
                    dve.wait_ge(k_transposed, total(i, k, 1, 0))
                for half, bank in enumerate((XA, XB)):
                    V.tensor_tensor(qk[:, 2 * half:2 * half + 2, :].rearrange("p a (h d) -> p (a h) d", d=DH),
                                    bank.rearrange("p (a d) -> p a d", d=DH),
                                    rs[:, 8 * half:8 * half + 8].unsqueeze(2).to_broadcast([P, 8, DH]),
                                    ALU.mult).then_inc(qk_scaled, 1)

            def low(dst, src, scale, hi, done):
                V.scalar_tensor_tensor(dst, src, scale, hi.bitcast(F32), ALU.mult, ALU.subtract).then_inc(done, 1)

            def low_q(i, k):
                dve.wait_ge(qt_hi_ready, total(i, k, 1, 1))
                low(qt_lo[:, k % 2, :], XB, scale_qk[:, 0, k % PAIRS:k % PAIRS + 1], qt_hi[:, k % 2, :], qt_ready)

            def low_k(i, k):
                dve.wait_ge(kt_hi_ready, total(i, k, 1, 1))
                low(kt_lo[:, k % 2, :], XA, scale_qk[:, 1, k % PAIRS:k % PAIRS + 1], kt_hi[:, k % 2, :], kt_ready)

            def low_xt(n):
                dve.wait_ge(xt_hi_ready, n)
                low(xt_lo[:], DEN, norm_col[:, 0:1], xt_hi[:], xt_ready)

            def normalise(i, k):
                dve.wait_ge(den_done, total(i, k, 1, 1))
                steps.after(V.transpose(den_t[:], DEN))
                steps.after(V.reciprocal(den_r[:], den_t[:].rearrange("p (a b) -> p a b", b=32)[:, :, 0]))
                steps.after(V.transpose(den_t[:].rearrange("p (a b) -> p a b", b=32),
                                        den_r[:].unsqueeze(2).to_broadcast([P, SEQ // 32, 32])))
                V.tensor_tensor(at[:, k % PAIRS, :], AV, den_t[:], ALU.mult).then_inc(at_ready, 1)
                dve.wait_ge(at_ready, total(i, k, 1, 1))

            def x_squares(b):
                rows_squares(x[:, bass.ds(b * QT, QT), :], EPS_ATTN)

            def x_hat(b):
                rows = x[:, bass.ds(b * QT, QT), :]
                rsqrt(ROW_COLS)
                V.tensor_tensor(xh[:], rows, rs[:, ROW_COLS].unsqueeze(2).to_broadcast([P, QT, D]),
                                ALU.mult).then_inc(xh_ready, 1)

            def residual(b, n, transposed):
                dve.wait_ge(xt_transposed, transposed)
                dve.wait_ge(wo_done, n)
                V.tensor_tensor(xh[:].rearrange("p a b -> p (a b)"),
                                x[:, bass.ds(b * QT, QT), :].rearrange("p a b -> p (a b)"), DEN,
                                ALU.add).then_inc(x1_ready, 1)

            def layer_norm_1(b, n):
                dve.wait_ge(x1_ready, n)
                centre(xh[:], den_t[:].rearrange("p (a b) -> p a b", b=D))
                steps.after(V.tensor_tensor(x[:, bass.ds(b * QT, QT), :], xh[:],
                                            rs[:, ROW_COLS].unsqueeze(2).to_broadcast([P, QT, D]), ALU.mult))

            def router_squares(b):
                rows_squares(x[:, bass.ds(b * QT, QT), :], EPS_FFN)

            def router_rows(b, n):
                dve.wait_ge(xq_free, n)
                rows = x[:, bass.ds(b * QT, QT), :]
                rsqrt(ROW_COLS)
                V.tensor_tensor(xq[:], rows, rs[:, ROW_COLS].unsqueeze(2).to_broadcast([P, QT, D]),
                                ALU.mult).then_inc(xq_ready, 1)

            def choose(b, n):
                dve.wait_ge(logits_copied, n)
                lg, tp = logits[:, bass.ds(b * QT, QT), :], top[:, bass.ds(b * QT, QT)]
                steps.after(V.tensor_reduce(least[:], batch_logits[:], AX_X, ALU.max))
                V.tensor_copy(lg, batch_logits[:])
                V.tensor_copy(tp, least[:])
                steps.after(V.tensor_tensor(is_top[:], batch_logits[:], least[:].unsqueeze(2).to_broadcast([P, QT, EXPERTS]),
                                            ALU.is_equal))
                steps.after(V.scalar_tensor_tensor(
                    choice[:], is_top[:], -float(EXPERTS),
                    count[:, 0:EXPERTS].unsqueeze(1).to_broadcast([P, QT, EXPERTS]), ALU.mult, ALU.add))
                steps.after(V.tensor_reduce(least[:], choice[:], AX_X, ALU.min))
                V.tensor_tensor(hot[:].rearrange("p e t -> p t e"), choice[:],
                                least[:].unsqueeze(2).to_broadcast([P, QT, EXPERTS]), ALU.is_equal).then_inc(hot_ready, 1)

            def assign(b, n):
                flat = lambda a: a.rearrange("p e t -> p (e t)")
                dve.wait_ge(next_slot_ready, n)
                dve.wait_ge(ranks_copied, n)
                steps.after(V.tensor_tensor_scan(flat(incl[:]), flat(carry[:]), flat(tot), 0.0, ALU.mult, ALU.add))
                steps.after(V.tensor_tensor(rank[:], ranks[:, 0, :, :], incl[:], ALU.add))
                steps.after(V.tensor_tensor(rank[:], rank[:], tot, ALU.subtract))
                steps.after(V.tensor_tensor(rank[:], rank[:], next_slot[:].unsqueeze(2).to_broadcast([P, EXPERTS, QT]),
                                            ALU.add))
                steps.after(V.tensor_tensor(rank[:], rank[:], hot[:], ALU.mult))
                steps.after(V.tensor_reduce(slot_f[:], rank[:].rearrange("p e t -> p t e"), AX_X, ALU.add))
                steps.after(V.tensor_copy(slot[:, bass.ds(b * QT, QT)], slot_f[:]))
                V.tensor_copy(batch_slot[:], slot_f[:]).then_inc(slots_ready, 1)

            def body(i, k, prepare=True):
                c, done = k % PAIRS, k >= PAIRS
                n = batch(i, k)
                ahead = k < GROUPS - LEAD
                if c == 1 and done:
                    router_squares(batch(i, k, -1))
                if c == 4 and ahead:
                    x_squares(batch(i, k, 1))
                if prepare:
                    scale_heads(i, k + 2)
                if c == 0 and done:
                    residual(batch(i, k, -1), n, batch(i, k, 1))
                    layer_norm_1(batch(i, k, -1), n)
                if c == 1 and done:
                    router_rows(batch(i, k, -1), n)
                if c == 2 and done:
                    choose(batch(i, k, -1), n)
                if c == 3 and done:
                    assign(batch(i, k, -1), n)
                if c == 4 and ahead:
                    x_hat(batch(i, k, 1))
                if prepare:
                    low_q(i, k + 2)
                    low_k(i, k + 2)
                if c == 5 and ahead:
                    low_xt(batch(i, k, 2))
                normalise(i, k)

            dve.wait_ge(x0_loaded, 16)
            x_squares(0)
            x_hat(0)
            dve.wait_ge(cols_loaded, 64)
            V.tensor_scalar(scale_qk[:], gam[:], 1.0, DH ** 0.5, ALU.add, ALU.mult).then_inc(scale_ready, 1)
            low_xt(1)
            dve.wait_ge(w_split, 1)
            V.tensor_tensor(w_lo[:, 0, :], w_f[:, 0, :], w_hi[:, 0, :].bitcast(F32), ALU.subtract).then_inc(w_split, 1)
            V.memset(carry[:], 1.0).then_inc(scale_ready, 1)
            dve.wait_ge(scale_ready, 2)
            V.memset(carry[:, :, 0:1], 0.0)
            dve.wait_ge(made, 3)
            steps.after(V.tensor_copy(count[:], count_i[:]))
            V.tensor_scalar(tile_starts[:], count[:, 0:TILES], float(P), None, ALU.mult)
            V.tensor_scalar(first_slots[:], count[:, 0:EXPERTS], float(TOKENS), None, ALU.mult)
            V.tensor_scalar(next_slot[:], count[:, 0:EXPERTS], float(TOKENS), None, ALU.mult).then_inc(next_slot_ready, 1)
            dve.sem_inc(xq_free, 1)
            scale_heads(None, 0, first=True)
            low_q(None, 0)
            low_k(None, 0)
            dve.wait_ge(w_split, 3)
            V.tensor_tensor(w_lo[:, 1:PAIRS, :], w_f[:, 1:PAIRS, :], w_hi[:, 1:PAIRS, :].bitcast(F32),
                            ALU.subtract).then_inc(w_split, 1)
            scale_heads(None, 1)
            low_q(None, 1)
            low_k(None, 1)
            dve.wait_ge(x_loaded, 16)
            for k in range(LEAD):
                body(None, k)
            with dve.Fori(0, ROUNDS) as i:
                steps.restart()
                for k in range(LEAD, LEAD + PAIRS):
                    body(i, k)
            steps.restart()
            for k in range(GROUPS - LEAD, GROUPS):
                body(None, k, prepare=k + 2 < GROUPS)
            last = BATCHES - 1
            residual(last, BATCHES, BATCHES)
            layer_norm_1(last, BATCHES)
            router_squares(last)
            router_rows(last, BATCHES)
            choose(last, BATCHES)
            assign(last, BATCHES)

            et = lambda a: a.rearrange("p (e t) -> p e t", e=EXPERTS)
            dve.wait_ge(next_slot_ready, BATCHES + 1)
            steps.after(V.tensor_tensor(n_tiles[:], next_slot[:], first_slots[:], ALU.subtract))
            steps.after(V.tensor_tensor(et(ra), n_tiles[:].unsqueeze(2).to_broadcast([P, EXPERTS, TILES]),
                                        tile_starts[:].unsqueeze(1).to_broadcast([P, EXPERTS, TILES]), ALU.is_gt))
            steps.after(V.tensor_reduce(n_tiles[:], et(ra), AX_X, ALU.add))
            steps.after(V.tensor_tensor_scan(ends[:], ones[:, 0:EXPERTS], n_tiles[:], 0.0, ALU.mult, ALU.add))
            all_s = [P, SLOT_TILES, EXPERTS]
            steps.after(V.tensor_tensor(cmp_s, count[:, 0:SLOT_TILES].unsqueeze(2).to_broadcast(all_s),
                                        ends[:].unsqueeze(1).to_broadcast(all_s), ALU.is_ge))
            steps.after(V.tensor_reduce(owner_f[:], cmp_s, AX_X, ALU.add))
            steps.after(V.tensor_scalar(n_tiles[:], n_tiles[:], -1.0, float(TILES), ALU.mult, ALU.add))
            steps.after(V.tensor_tensor(cmp_n, cmp_s, n_tiles[:].unsqueeze(1).to_broadcast(all_s), ALU.mult))
            steps.after(V.tensor_reduce(place_f[:], cmp_n, AX_X, ALU.add))
            steps.after(V.tensor_tensor(place[:], place_f[:], count[:, 0:SLOT_TILES], ALU.add))
            V.tensor_scalar(owner[:], owner_f[:], float(EXPERTS - 1), None, ALU.min).then_inc(owners_ready, 1)
            dve.wait_ge(owners_ready, 1)
            te7 = lambda a: a[:, 0:TILES * (EXPERTS - 1)].rearrange("p (t e) -> p t e", e=EXPERTS - 1)
            by_token = [P, TILES, EXPERTS - 1]
            steps.after(V.tensor_tensor(te7(ra), slot[:].unsqueeze(2).to_broadcast(by_token),
                                        first_slots[:, 1:EXPERTS].unsqueeze(1).to_broadcast(by_token), ALU.is_ge))
            steps.after(V.tensor_tensor(te7(rb), te7(ra), n_tiles[:, 0:EXPERTS - 1].unsqueeze(1).to_broadcast(by_token),
                                        ALU.mult))
            steps.after(V.tensor_reduce(row_f[:], te7(rb), AX_X, ALU.add))
            steps.after(V.tensor_scalar(row_f[:], row_f[:], -float(P), None, ALU.mult))
            V.tensor_tensor(row[:], row_f[:], slot[:], ALU.add).then_inc(rows_known, 1)
            dve.wait_ge(rows_known, 1)
            dve.wait_ge(ffn_loaded, 64)

            def expert(s):
                return V.value_load(owner[0:1, bass.ds(s, 1)], min_val=0, max_val=EXPERTS - 1)

            def move_xst(s, m):
                dve.wait_ge(xs_transposed, s + 1)
                V.tensor_scalar(xst[m % 3], XST, rms_col[:, 0:1], None, ALU.mult).then_inc(xst_ready, 1)

            def hidden_pre(s, m):
                e = expert(s)
                dve.wait_ge(up_done, s + 1)
                V.tensor_tensor(pre[m % 3], U[m % 3], b_1[:, bass.ds(e, 1), :].rearrange("p a b -> p (a b)"),
                                ALU.add).then_inc(pre_ready, 1)

            def hidden(s, m):
                dve.wait_ge(th_ready, s + 1)
                V.scalar_tensor_tensor(hid[m % 3], th[m % 3], 1.0, pre[m % 3], ALU.add, ALU.mult).then_inc(hid_ready, 1)

            def tile_out(s, m, stored=None):
                e = expert(s)
                dve.wait_ge(down_done, s + 1)
                if stored is not None:
                    dve.wait_ge(y_stored[m % 3], stored)
                V.tensor_tensor(ys[m % 3], Y, b_2[:, bass.ds(e, 1), :].rearrange("p a b -> p (a b)"),
                                ALU.add).then_inc(y_ready, 1)

            def tile(s, m, stored=None, up2=True, up3=True):
                if up3:
                    move_xst(s + 3, m + 3)
                if up2:
                    hidden_pre(s + 2, m + 2)
                tile_out(s, m, stored)
                if up2:
                    hidden(s + 2, m + 2)

            for s in range(3):
                move_xst(s, s)
            for s in range(2):
                hidden_pre(s, s)
                hidden(s, s)
            for s in range(3):
                tile(s, s)
            with dve.Fori(1, SLOT_TILES // 3 - 1) as i:
                for m in range(3):
                    tile(i * 3 + m, m, stored=i * 16)
            for s in range(SLOT_TILES - 3, SLOT_TILES):
                tile(s, s, stored=16 * (s // 3), up2=s + 2 < SLOT_TILES, up3=False)

            te = lambda a: a.rearrange("p (t e) -> p t e", e=EXPERTS)
            V.tensor_tensor(te(ra), logits[:], top[:].unsqueeze(2).to_broadcast([P, TILES, EXPERTS]),
                            ALU.subtract).then_inc(shifted_ready, 1)
            dve.wait_ge(score_exp_done, 1)
            steps.after(V.tensor_reduce(score[:], te(rb), AX_X, ALU.add))
            steps.after(V.reciprocal(score[:], score[:]))

            for n in range(TILES // QT):
                tiles = range(QT * n, QT * n + QT)
                dve.wait_ge(gathered[n], 16 * QT)
                for t in tiles:
                    last = V.scalar_tensor_tensor(yr[:, t, :], yr[:, t, :], score[:, t:t + 1], x[:, t, :], ALU.mult, ALU.add)
                steps.after(last)
                for m, t in enumerate(tiles):
                    last = V.bn_stats(stats[:, m, :], yr[:, t, :])
                steps.after(last)
                for m in range(QT):
                    last = V.bn_aggr(mv[:, m, :], stats[:, m, :])
                steps.after(last)
                steps.after(V.tensor_scalar(ss[:, ROW_COLS], mv[:, :, 1], 1.0, EPS_LN, ALU.mult, ALU.add))
                rsqrt(ROW_COLS)
                for m, t in enumerate(tiles):
                    last = V.tensor_scalar(yr[:, t, :], yr[:, t, :], mv[:, m, 0:1], rs[:, 16 + m:17 + m], ALU.subtract, ALU.mult)
                last.then_inc(out_ready, 1)
                dve.wait_ge(out_ready, n + 1)

        @block.tensor
        def _(pe):
            mm = nc.tensor.matmul

            def split_mm(out_, lhs_hi, lhs_lo, rhs_hi, rhs_lo):
                mm(out_, lhs_lo, rhs_hi, start=True, stop=False)
                mm(out_, lhs_hi, rhs_lo, start=False, stop=False)
                return mm(out_, lhs_hi, rhs_hi, start=False, stop=True)

            def project_qk(i, k, b, first=False):
                pe.wait_ge(xt_ready, b)
                if not first:
                    pe.wait_ge(kt_ready, total(i, k, 1, 0))
                    pe.wait_ge(qt_ready, total(i, k, 1, 0))
                c = k % PAIRS
                for t in range(QT):
                    rows = slice(t * P, (t + 1) * P)
                    last = split_mm(ps[:, 6 + t // 2, (t % 2) * 256:(t % 2) * 256 + 256], xt_hi[:, rows], xt_lo[:, rows],
                                    w_hi[:, c, 0:2 * P], w_lo[:, c, 0:2 * P])
                last.then_inc(qk_projected, 1)

            def project_v(k, half):
                c = k % PAIRS
                for t in (0, 1):
                    rows = slice((2 * half + t) * P, (2 * half + t + 1) * P)
                    last = split_mm(DEN[:, t * 2 * P:(t + 1) * 2 * P], xt_hi[:, rows], xt_lo[:, rows],
                                    w_hi[:, c:c + 2, 2 * P:3 * P], w_lo[:, c:c + 2, 2 * P:3 * P])
                last.then_inc(v_projected, 1)

            def transpose_qk(i, k):
                pe.wait_ge(qk_scaled, total(i, k, 2, 2))
                for bank, cols, done in ((XB, slice(0, P), q_transposed), (XA, slice(P, 2 * P), k_transposed)):
                    for t in range(QT):
                        last = nc.tensor.transpose(bank[:, t * P:(t + 1) * P], qk[:, t, cols], ident[:])
                    last.then_inc(done, 1)

            def scores(i, k, j, fresh=False):
                if j == 0:
                    pe.wait_ge(qt_ready, total(i, k, 1, 1))
                    pe.wait_ge(kt_ready, total(i, k, 1, 1))
                if not fresh:
                    pe.wait_ge(tanh_done, total(i, k, 4, j - 1))
                for h in range(2):
                    rows, keys = slice(DH * h, DH * (h + 1)), slice(j * P, (j + 1) * P)
                    last = split_mm(S[j % 2][:, h, :], kt_hi[rows, k % 2, keys], kt_lo[rows, k % 2, keys],
                                    qt_hi[rows, k % 2, :], qt_lo[rows, k % 2, :])
                last.then_inc(scored, 1)

            def pv(i, k, j, first=False):
                if j % 2 == 0:
                    pe.wait_ge(exp_done, total(i, k, 2, j // 2 + 1))
                if j == 0:
                    if first:
                        pe.wait_ge(v_copied, 2)
                    else:
                        pe.wait_ge(at_ready, total(i, k, 1, 0))
                for h in range(2):
                    last = mm(AV[DH * h:DH * (h + 1), :], v[:, k % 4, j, DH * h:DH * (h + 1)],
                              pr[:, k % 2, j, h * SEQ:(h + 1) * SEQ], start=j == 0, stop=j == QT - 1)
                if j == QT - 1:
                    last.then_inc(pv_done, 1)

            def softmax_sums(i, k):
                pe.wait_ge(sums_ready, total(i, k, 1, 1))
                for h in range(2):
                    last = mm(DEN[DH * h:DH * (h + 1), :], ones[:, 0:DH], sums[:, h * SEQ:(h + 1) * SEQ],
                              start=True, stop=True)
                last.then_inc(den_done, 1)

            def output_projection(n):
                for t in range(QT):
                    for c in range(PAIRS):
                        last = mm(DEN[:, t * D:(t + 1) * D], at[:, c, t * P:(t + 1) * P], w_o[:, c, :],
                                  start=c == 0, stop=c == PAIRS - 1)
                last.then_inc(wo_done, 1)

            def transpose_rows(rows, done):
                for t in range(QT):
                    last = nc.tensor.transpose(DEN[:, t * P:(t + 1) * P], rows[:, t, :], ident[:])
                last.then_inc(done, 1)

            def router_logits(n):
                pe.wait_ge(xrt_ready, n)
                for t in range(QT):
                    last = mm(DEN[:, t * EXPERTS:(t + 1) * EXPERTS], xrt[:, t * P:(t + 1) * P], gate_t[:],
                              start=True, stop=True)
                last.then_inc(logits_done, 1)

            def rank_tokens(n):
                pe.wait_ge(hot_ready, n)
                w, hots = QT * EXPERTS, hot[:].rearrange("p e t -> p (e t)")
                mm(DEN[:, 0:w], before[:], hots, start=True, stop=True)
                mm(DEN[:, w:2 * w], ones[:], hots, start=True, stop=True).then_inc(ranked, 1)

            def body(i, k, first=False):
                c, done = k % PAIRS, k >= PAIRS
                prepare, score_next = k + 2 < GROUPS, k + 1 < GROUPS
                n = batch(i, k)
                if score_next:
                    scores(i, k + 1, 0)
                if prepare:
                    project_qk(i, k + 2, batch(i, k + 2, 1))
                if score_next:
                    scores(i, k + 1, 1)
                pv(i, k, 0, first)
                if c == 0 and done:
                    output_projection(n)
                if c == 2 and done:
                    router_logits(n)
                if c == 3 and done:
                    rank_tokens(n)
                pv(i, k, 1)
                if score_next:
                    scores(i, k + 1, 2)
                pv(i, k, 2)
                if done and c in (0, 2, 3):
                    pe.wait_ge({0: x1_ready, 2: logits_copied, 3: ranks_copied}[c], n)
                if prepare:
                    project_v(k + 2 - k % 2, k % 2)
                    transpose_qk(i, k + 2)
                if score_next:
                    scores(i, k + 1, 3)
                if prepare:
                    pe.wait_ge(v_copied, total(i, k, 1, 3))
                if c == 1 and done:
                    pe.wait_ge(xq_ready, n)
                    transpose_rows(xq, xq_transposed)
                if c == 5 and k < GROUPS - LEAD:
                    pe.wait_ge(xh_ready, batch(i, k, 2))
                    transpose_rows(xh, xt_transposed)
                pv(i, k, 3)
                if c == 1 and done:
                    pe.wait_ge(xrt_ready, n)
                if c == 5 and k < GROUPS - LEAD:
                    pe.wait_ge(xt_ready, batch(i, k, 2))
                softmax_sums(i, k)

            pe.wait_ge(consts_ready, 2)
            pe.wait_ge(xh_ready, 1)
            transpose_rows(xh, xt_transposed)
            pe.wait_ge(w_split, 2)
            project_qk(None, 0, 1, first=True)
            transpose_qk(None, 0)
            pe.wait_ge(w_split, 4)
            project_qk(None, 1, 1)
            scores(None, 0, 0, fresh=True)
            scores(None, 0, 1, fresh=True)
            project_v(0, 0)
            scores(None, 0, 2)
            transpose_qk(None, 1)
            pe.wait_ge(v_copied, 1)
            project_v(0, 1)
            scores(None, 0, 3)
            pe.wait_ge(wo_loaded, 32)
            for k in range(LEAD):
                body(None, k, first=k == 0)
            with pe.Fori(0, ROUNDS) as i:
                for k in range(LEAD, LEAD + PAIRS):
                    body(i, k)
            for k in range(GROUPS - LEAD, GROUPS):
                body(None, k)

            pe.wait_ge(at_ready, GROUPS)
            output_projection(BATCHES)
            pe.wait_ge(xq_ready, BATCHES)
            transpose_rows(xq, xq_transposed)
            router_logits(BATCHES)
            rank_tokens(BATCHES)

            def expert(s):
                return nc.tensor.value_load(owner[0:1, bass.ds(s, 1)], min_val=0, max_val=EXPERTS - 1)

            def transpose_x(m, loaded):
                pe.wait_ge(xs_loaded[m % 3], loaded)
                nc.tensor.transpose(XST, xs[m % 3], ident[:]).then_inc(xs_transposed, 1)

            def up(s, m, fresh=False):
                e = expert(s)
                pe.wait_ge(xst_ready, s + 1)
                if not fresh:
                    pe.wait_ge(pre_ready, s - 2)
                mm(U[m % 3], xst[m % 3], w_1[:, bass.ds(e, 1), :].rearrange("p a b -> p (a b)"),
                   start=True, stop=True).then_inc(up_done, 1)

            def tile(s, m, loaded=None, first=False, ahead2=True):
                pe.wait_ge(hid_ready, s + 1)
                if not first:
                    pe.wait_ge(ht_copied, s)
                for f in range(FK):
                    last = nc.tensor.transpose(HT[:, f * P:(f + 1) * P], hid[m % 3][:, f * P:(f + 1) * P], ident[:])
                last.then_inc(h_transposed, 1)
                if ahead2:
                    up(s + 2, m + 2, fresh=first)
                if loaded is not None:
                    pe.wait_ge(xst_ready, s + 3)
                    transpose_x(m + 3, loaded)
                e = expert(s)
                pe.wait_ge(ht_copied, s + 1)
                if not first:
                    pe.wait_ge(y_ready, s)
                for f in range(FK):
                    last = mm(Y, ht_sb[:, f * P:(f + 1) * P],
                              w_2[:, bass.ds(e, 1), f * D:(f + 1) * D].rearrange("p a b -> p (a b)"),
                              start=f == 0, stop=f == FK - 1)
                last.then_inc(down_done, 1)

            pe.wait_ge(owners_ready, 1)
            pe.wait_ge(ffn_loaded, 64)
            for s in range(3):
                if s:
                    pe.wait_ge(xst_ready, s)
                transpose_x(s, 16)
            up(0, 0, fresh=True)
            up(1, 1, fresh=True)
            for s in range(3):
                tile(s, s, loaded=32, first=s == 0)
            with pe.Fori(1, SLOT_TILES // 3 - 1) as i:
                for m in range(3):
                    tile(i * 3 + m, m, loaded=i * 16 + 32)
            for s in range(SLOT_TILES - 3, SLOT_TILES):
                tile(s, s, ahead2=s + 2 < SLOT_TILES)


_ORDER = ["tokens", "norm_w", "wq", "wkv", "wo", "q_gamma", "k_gamma", "rms_w", "gate_w", "w1", "b1", "w2", "b2"]


def kernel(L0_attn_tokens, L0_attn_norm_w, L0_attn_Wq, L0_attn_Wkv, L0_attn_Wo, L0_attn_q_gamma,
           L0_attn_k_gamma, L0_ffn_rms_w, L0_ffn_gate_w, L0_ffn_W1, L0_ffn_b1, L0_ffn_W2, L0_ffn_b2):
    import numpy as np
    import concourse.bacc as bacc
    from concourse.bass_utils import run_bass_kernel_spmd

    def column(a):
        return np.ascontiguousarray(np.asarray(a).reshape(-1, P).T)

    arrays = dict(
        tokens=np.asarray(L0_attn_tokens).reshape(TOKENS, D),
        norm_w=column(L0_attn_norm_w), wq=np.asarray(L0_attn_Wq), wkv=np.asarray(L0_attn_Wkv),
        wo=np.asarray(L0_attn_Wo), q_gamma=column(L0_attn_q_gamma), k_gamma=column(L0_attn_k_gamma),
        rms_w=column(L0_ffn_rms_w), gate_w=np.ascontiguousarray(np.asarray(L0_ffn_gate_w).T),
        w1=np.asarray(L0_ffn_W1), b1=np.asarray(L0_ffn_b1).reshape(1, -1),
        w2=np.asarray(L0_ffn_W2), b2=np.asarray(L0_ffn_b2).reshape(1, -1),
    )
    nc = bacc.Bacc("TRN2", target_bir_lowering=False, num_devices=1)
    args = [nc.dram_tensor(f"in_{n}", arrays[n].shape, F32, kind="ExternalInput").ap() for n in _ORDER]
    out = nc.dram_tensor("out", [TOKENS, D], F32, kind="ExternalOutput").ap()
    build(nc, *args, out)
    r = run_bass_kernel_spmd(nc, [{f"in_{n}": np.ascontiguousarray(arrays[n]) for n in _ORDER}], core_ids=[0])
    return r.results[0]["out"].reshape(BATCHES, SEQ, D)
```

```python
from contextlib import ExitStack

import concourse.bass as bass
import concourse.mybir as mybir

F32 = mybir.dt.float32
F32R = mybir.dt.float32r
I32 = mybir.dt.int32
ALU = mybir.AluOpType
ACT = mybir.ActivationFunctionType
AX_X = mybir.AxisListType.X

P = 128
D = 128
HEADS, DH = 16, 64
BATCHES, SEQ = 8, 512
TOKENS = BATCHES * SEQ
PAIRS = HEADS // 2
GROUPS = BATCHES * PAIRS
QT = SEQ // P
TILES = TOKENS // P
EXPERTS, FF = 8, 512
FK = FF // P
PART_TOKEN_TILES = (TILES - QT, QT)
PART_SLOT_TILES = tuple(t + EXPERTS - 1 for t in PART_TOKEN_TILES)
A_TILES, SLOT_TILES = PART_SLOT_TILES[0], sum(PART_SLOT_TILES)
PART_DRAM_TILES = tuple(EXPERTS * t + EXPERTS - 1 for t in PART_TOKEN_TILES)
DRAM_TILES = sum(PART_DRAM_TILES)
LEAD_TILES = 15
ROUND_TILES = 9
LOOP_ROUNDS = (A_TILES - LEAD_TILES) // ROUND_TILES
REST_TILES = range(LEAD_TILES + LOOP_ROUNDS * ROUND_TILES, SLOT_TILES)
ZERO_TILES = 32
ZEROS_STORED = 16 * -(-DRAM_TILES // ZERO_TILES)
CLAMP = 50.0
EPS_ATTN = 1.1920928955078125e-07
EPS_FFN = 1e-6
EPS_LN = 1e-5
TINY = 1e-24
NORM_CHUNKS = [range(0, 4 * QT), range(4 * QT, 7 * QT), range(7 * QT, 8 * QT)]
RSQRT_MAGIC = float(0x5F3759DF)


class Steps:

    def __init__(self, engine, sem):
        self.engine, self.sem, self.n = engine, sem, 0

    def restart(self):
        self.engine.sem_clear(self.sem)
        self.n = 0

    def after(self, instruction):
        instruction.then_inc(self.sem, 1)
        self.n += 1
        self.engine.wait_ge(self.sem, self.n)


def build(nc, tokens, norm_w, wq, wkv, wo, q_gamma, k_gamma, rms_w, gate_w, w1, b1, w2, b2, out):
    sorted_x = nc.dram_tensor("sorted_x", [DRAM_TILES * P, D], F32, kind="Internal").ap()
    sorted_ys = [nc.dram_tensor(f"sorted_y{part}", [n * P, D], F32, kind="Internal").ap()
                 for part, n in enumerate(PART_SLOT_TILES)]

    with ExitStack() as ctx:
        def sb(name, shape, dt=F32):
            return ctx.enter_context(nc.sbuf_tensor(name, shape, dt))

        def sem(name):
            return ctx.enter_context(nc.semaphore(name))

        w_hi = sb("w_hi", [P, PAIRS, 3 * P], F32R)
        w_lo = sb("w_lo", [P, PAIRS, 3 * P], F32R)
        w_o = sb("w_o", [P, PAIRS, D])
        w_1 = sb("w_1", [P, EXPERTS, FF])
        w_2 = sb("w_2", [P, EXPERTS, FK * D])
        b_1 = sb("b_1", [P, EXPERTS, FF])
        b_2 = sb("b_2", [P, EXPERTS, D])
        gate_t = sb("gate_t", [P, EXPERTS])
        norm_col = sb("norm_col", [P, 1])
        rms_col = sb("rms_col", [P, 1])
        gam = sb("gam", [P, 2, PAIRS])
        scale_qk = sb("scale_qk", [P, 2, PAIRS])
        ident = sb("ident", [P, P])
        ones = sb("ones", [P, P])
        before = sb("before", [P, P])
        count_i = sb("count_i", [P, 64], I32)
        count = sb("count", [P, 64])
        tile_starts = sb("tile_starts", [P, TILES])
        first_slots = sb("first_slots", [P, 2, EXPERTS])
        carry = sb("carry", [P, EXPERTS, QT])
        zeros = b_1[:].rearrange("p e f -> p (e f)")

        x = sb("x", [P, TILES, D])
        xh = sb("xh", [P, QT, D])
        xq = sb("xq", [P, QT, D])
        xt_hi = sb("xt_hi", [P, SEQ], F32R)
        xt_lo = sb("xt_lo", [P, SEQ], F32R)
        sq = sb("sq", [P, 4, 2 * P])
        qk = sb("qk", [P, QT, 2 * P])
        qt_hi = sb("qt_hi", [P, 2, SEQ], F32R)
        qt_lo = sb("qt_lo", [P, 2, SEQ], F32R)
        kt_hi = sb("kt_hi", [P, 2, SEQ], F32R)
        kt_lo = sb("kt_lo", [P, 2, SEQ], F32R)
        v = sb("v", [P, 4, QT, P])
        pr = sb("pr", [P, 2, QT, 2 * SEQ])
        pair_sums = sb("pair_sums", [P, 2, 2 * SEQ])
        sums = sb("sums", [P, 2 * SEQ])
        den_t = sb("den_t", [P, SEQ])
        den_r = sb("den_r", [P, SEQ // 32])
        at = sb("at", [P, PAIRS, SEQ])
        xrt = sb("xrt", [P, SEQ])
        ss = sb("ss", [P, 64])
        rs = sb("rs", [P, 64])
        na = sb("na", [P, 64])
        stats = sb("stats", [P, QT, 6])
        mv = sb("mv", [P, TILES, 2])
        nb = sb("nb", [P, 64])
        warm = sb("warm", [P, 1])

        logits = sb("logits", [P, TILES, EXPERTS])
        top = sb("top", [P, TILES])
        is_top = sb("is_top", [P, QT, EXPERTS])
        choice = sb("choice", [P, QT, EXPERTS])
        least = sb("least", [P, QT])
        hot = sb("hot", [P, EXPERTS, QT])
        batch_logits = sb("batch_logits", [P, QT, EXPERTS])
        ranks = sb("ranks", [P, 2, EXPERTS, QT])
        tot = ranks[:, 1, :, :]
        incl = sb("incl", [P, EXPERTS, QT])
        rank = sb("rank", [P, EXPERTS, QT])
        slot_f = sb("slot_f", [P, QT])
        batch_slot = sb("batch_slot", [P, QT], I32)
        next_slot = sb("next_slot", [P, EXPERTS])
        slot = sb("slot", [P, TILES], I32)
        score = sb("score", [P, TILES])
        row_f = sb("row_f", [P, TILES])
        row = sb("row", [P, TILES], I32)
        n_tiles = sb("n_tiles", [P, EXPERTS])
        ends = sb("ends", [P, EXPERTS])
        owner_f = sb("owner_f", [P, A_TILES])
        owner = sb("owner", [P, SLOT_TILES], I32)
        place_f = sb("place_f", [P, A_TILES])
        place = sb("place", [P, SLOT_TILES], I32)
        sq_flat = sq[:].rearrange("p a b -> p (a b)")
        ra, rb = sq_flat[:, 0:TILES * EXPERTS], sq_flat[:, TILES * EXPERTS:2 * TILES * EXPERTS]
        cmp_n, cmp_s = sq_flat[:, 0:A_TILES * EXPERTS], sq_flat[:, 2 * TILES * EXPERTS:(2 * TILES + A_TILES) * EXPERTS]

        w_f = pr[:, 1, :, :].rearrange("p a b -> p (a b)")[:, 0:PAIRS * 3 * P].rearrange("p (c n) -> p c n", c=PAIRS)

        p0 = pr[:, 0, :, :].rearrange("p a b -> p (a b)")
        p1 = pr[:, 1, :, :].rearrange("p a b -> p (a b)")
        pre = [p0[:, m * FF:(m + 1) * FF] for m in range(3)]
        hid = [p0[:, (3 + m) * FF:(4 + m) * FF] for m in range(3)]
        xs = [p0[:, 6 * FF + m * P:6 * FF + (m + 1) * P] for m in range(3)]
        xst = [p0[:, 6 * FF + (3 + m) * P:6 * FF + (4 + m) * P] for m in range(3)]
        th = [p1[:, m * FF:(m + 1) * FF] for m in range(3)]
        ht_sb = p1[:, 3 * FF:4 * FF]
        ys = [p1[:, 4 * FF + m * P:4 * FF + (m + 1) * P] for m in range(3)]
        yr = at[:].rearrange("p c n -> p (c n)").rearrange("p (t d) -> p t d", d=D)

        ps = ctx.enter_context(nc.psum_tensor("ps", [P, 8, 512], F32))
        S = [ps[:, 2 * k:2 * k + 2, :] for k in range(2)]
        AV, DEN, XA, XB = ps[:, 4, :], ps[:, 5, :], ps[:, 6, :], ps[:, 7, :]
        U = [ps[:, m, :] for m in range(3)]
        HT, Y, XST = ps[:, 3, :], ps[:, 4, 0:D], ps[:, 6, 0:P]

        x0_loaded, x_loaded = sem("x0_loaded"), sem("x_loaded")
        w_first_loaded, w_loaded, cols_loaded = sem("w_first_loaded"), sem("w_loaded"), sem("cols_loaded")
        wo_loaded, ffn_loaded = sem("wo_loaded"), sem("ffn_loaded")
        w_first_split, w_split = sem("w_first_split"), sem("w_split")
        zeroed = sem("zeroed")
        zeros_stored = sem("zeros_stored")
        made, consts_ready, scale_ready = sem("made"), sem("consts_ready"), sem("scale_ready")
        dve_steps, pool_steps = sem("dve_steps"), sem("pool_steps")
        xh_ready, xt_transposed = sem("xh_ready"), sem("xt_transposed")
        xt_hi_ready, xt_ready = sem("xt_hi_ready"), sem("xt_ready")
        qk_projected = sem("qk_projected")
        squared, qk_scaled = sem("squared"), sem("qk_scaled")
        squares_summed = sem("squares_summed")
        v_projected, v_copied = sem("v_projected"), sem("v_copied")
        q_transposed, qt_hi_ready, qt_ready = sem("q_transposed"), sem("qt_hi_ready"), sem("qt_ready")
        k_transposed, kt_hi_ready, kt_ready = sem("k_transposed"), sem("kt_hi_ready"), sem("kt_ready")
        scored, tanh_done, exp_done = sem("scored"), sem("tanh_done"), sem("exp_done")
        pv_done, sums_ready, den_done, at_ready = sem("pv_done"), sem("sums_ready"), sem("den_done"), sem("at_ready")
        wo_done, x1_ready = sem("wo_done"), sem("x1_ready")
        xq_ready, xq_transposed, xrt_ready = sem("xq_ready"), sem("xq_transposed"), sem("xrt_ready")
        logits_done, logits_copied = sem("logits_done"), sem("logits_copied")
        hot_ready, ranked, ranks_copied = sem("hot_ready"), sem("ranked"), sem("ranks_copied")
        slots_ready = sem("slots_ready")
        next_slot_ready, xq_free = sem("next_slot_ready"), sem("xq_free")
        scattered = sem("scattered")
        rows_known, owners_ready = sem("rows_known"), sem("owners_ready")
        shifted_ready, score_exp_done = sem("shifted_ready"), sem("score_exp_done")
        xs_loaded = [sem(f"xs_loaded{m}") for m in range(3)]
        y_stored = [sem(f"y_stored{m}") for m in range(3)]
        xs_transposed, xst_ready, up_done = sem("xs_transposed"), sem("xst_ready"), sem("up_done")
        pre_ready, th_ready, hid_ready = sem("pre_ready"), sem("th_ready"), sem("hid_ready")
        h_transposed, ht_copied, down_done, y_ready = sem("h_transposed"), sem("ht_copied"), sem("down_done"), sem("y_ready")
        gathered = [sem(f"gathered{n}") for n in range(TILES // QT)]
        norm_ready, last_out_ready = sem("norm_ready"), sem("last_out_ready")
        out_ready, out_stored = sem("out_ready"), sem("out_stored")

        block = ctx.enter_context(nc.Block())

        LEAD = 4
        ROUNDS = BATCHES - 1

        def total(i, k, each, plus):
            n = each * k + plus
            return n if i is None else i * (each * PAIRS) + n

        def batch(i, k, plus=0):
            n = k // PAIRS + plus
            return n if i is None else i + n

        def experts(engine, s, n):
            _, values = nc.values_load_multi_w_load_instructions(
                owner[0:1, bass.ds(s, n)], engines=[engine], min_val=0, max_val=EXPERTS - 1)
            return values

        @block.sync
        def _(sp):
            xv = tokens.rearrange("(t p) d -> p t d", p=P)
            sp.dma_start(x[:, 0:QT, :], xv[:, 0:QT, :]).then_inc(x0_loaded, 16)
            for n, w in enumerate((wq, wkv[:, 0:HEADS * DH], wkv[:, HEADS * DH:2 * HEADS * DH])):
                sp.dma_start(w_f[:, 0:2, n * P:(n + 1) * P],
                             w[:, 0:2 * P].rearrange("d (c n) -> d c n", n=P)).then_inc(w_first_loaded, 16)
            sp.dma_start(norm_col[:], norm_w).then_inc(cols_loaded, 16)
            sp.dma_start(gam[:, 0, :], q_gamma).then_inc(cols_loaded, 16)
            sp.dma_start(gam[:, 1, :], k_gamma).then_inc(cols_loaded, 16)
            sp.dma_start(rms_col[:], rms_w).then_inc(cols_loaded, 16)
            for n, w in enumerate((wq, wkv[:, 0:HEADS * DH], wkv[:, HEADS * DH:2 * HEADS * DH])):
                sp.dma_start(w_f[:, 2:PAIRS, n * P:(n + 1) * P],
                             w[:, 2 * P:PAIRS * P].rearrange("d (c n) -> d c n", n=P)).then_inc(w_loaded, 16)
            sp.dma_start(x[:, QT:TILES, :], xv[:, QT:TILES, :]).then_inc(x_loaded, 16)
            sp.dma_start(w_o[:], wo.rearrange("(c p) n -> p c n", p=P)).then_inc(wo_loaded, 16)
            sp.dma_start(gate_t[:], gate_w).then_inc(wo_loaded, 16)
            sp.wait_ge(zeroed, 1)
            zv = sorted_x.rearrange("(p t) d -> p (t d)", p=P)
            for t in range(0, DRAM_TILES, ZERO_TILES):
                n = min(ZERO_TILES, DRAM_TILES - t) * D
                sp.dma_start(zv[:, t * D:t * D + n], zeros[:, 0:n]).then_inc(zeros_stored, 16)
            sp.dma_start(w_1[:], w1.rearrange("e d f -> d e f")).then_inc(ffn_loaded, 16)
            sp.dma_start(w_2[:].rearrange("p e (k n) -> p (e k) n", k=FK),
                         w2.rearrange("e (k p) n -> p (e k) n", p=P)).then_inc(ffn_loaded, 16)
            sp.wait_ge(zeros_stored, ZEROS_STORED)
            sp.dma_start(b_1[:].rearrange("p e f -> p (e f)"), b1.to_broadcast([P, EXPERTS * FF])).then_inc(ffn_loaded, 16)
            sp.dma_start(b_2[:].rearrange("p e f -> p (e f)"), b2.to_broadcast([P, EXPERTS * D])).then_inc(ffn_loaded, 16)

            def load(s, m):
                t = sp.value_load(place[0:1, bass.ds(s, 1)], min_val=0, max_val=DRAM_TILES - 1)
                sp.dma_start(xs[m % 3], sorted_x[bass.ds(t * P, P), :]).then_inc(xs_loaded[m % 3], 16)

            sp.wait_ge(owners_ready, 1)
            sp.wait_ge(scattered, 16 * PART_TOKEN_TILES[0])
            sp.wait_ge(pv_done, GROUPS - 1)
            sp.wait_ge(sums_ready, GROUPS - 1)
            for m in range(3):
                load(m, m)
            with sp.Fori(1, A_TILES // 3) as i:
                for m in range(3):
                    sp.wait_ge(xs_transposed, i * 3 + m - 2)
                    load(i * 3 + m, m)
            for s in range(A_TILES - A_TILES % 3, A_TILES):
                sp.wait_ge(xs_transposed, s - 2)
                load(s, s)
            sp.wait_ge(owners_ready, 2)
            sp.wait_ge(scattered, 16 * TILES)
            for s in range(A_TILES, SLOT_TILES):
                sp.wait_ge(xs_transposed, s - 2)
                load(s, s)
            ov = out.rearrange("(t p) d -> p t d", p=P)
            for b in range(BATCHES):
                if b < BATCHES - 1:
                    sp.wait_ge(out_ready, b + 1)
                else:
                    sp.wait_ge(last_out_ready, 1)
                w = slice(b * QT, (b + 1) * QT)
                sp.dma_start(ov[:, w, :], yr[:, w, :]).then_inc(out_stored, 16)
            sp.wait_ge(out_stored, 16 * BATCHES)

        @block.gpsimd
        def _(pool):
            steps = Steps(pool, pool_steps)
            nc.gpsimd.memset(ident[:], 0.0).then_inc(made, 1)
            nc.gpsimd.memset(ones[:], 1.0).then_inc(made, 1)
            nc.gpsimd.iota(count_i[:], pattern=[[1, 64]], base=0, channel_multiplier=0).then_inc(made, 1)
            pool.wait_ge(made, 3)
            nc.gpsimd.affine_select(out=ident[:], in_=ident[:], compare_op=ALU.not_equal, fill=1.0, base=0,
                                    pattern=[[-1, P]], channel_multiplier=1).then_inc(consts_ready, 1)
            nc.gpsimd.affine_select(out=before[:], in_=ones[:], compare_op=ALU.is_gt, fill=0.0, base=0,
                                    pattern=[[1, P]], channel_multiplier=-1).then_inc(consts_ready, 1)
            nc.gpsimd.memset(zeros, 0.0).then_inc(zeroed, 1)

            def body(i, k, first=False):
                pair = pr[:, k % 2, :, :]
                pool.wait_ge(exp_done, total(i, k, 2, 1))
                steps.after(nc.gpsimd.tensor_tensor(pair_sums[:, 0, :], pair[:, 0, :], pair[:, 1, :], ALU.add))
                pool.wait_ge(exp_done, total(i, k, 2, 2))
                steps.after(nc.gpsimd.tensor_tensor(pair_sums[:, 1, :], pair[:, 2, :], pair[:, 3, :], ALU.add))
                if not first:
                    pool.wait_ge(den_done, total(i, k, 1, 0))
                nc.gpsimd.tensor_tensor(sums[:], pair_sums[:, 0, :], pair_sums[:, 1, :], ALU.add).then_inc(sums_ready, 1)
                if k % PAIRS == 3 and k > PAIRS:
                    scatter(batch(i, k))
                pool.wait_ge(sums_ready, total(i, k, 1, 1))

            def scatter(n):
                pool.wait_ge(slots_ready, n)
                nc.gpsimd.tensor_tensor(next_slot[:], next_slot[:], incl[:, :, QT - 1], ALU.add).then_inc(next_slot_ready, 1)
                pool.wait_ge(zeros_stored, ZEROS_STORED)
                for t in range(QT):
                    nc.gpsimd.indirect_dma_start(
                        out=sorted_x, out_offset=bass.IndirectOffsetOnAxis(ap=batch_slot[:, t:t + 1], axis=0),
                        in_=xq[:, t, :], in_offset=None).then_inc(scattered, 16)
                pool.wait_ge(scattered, n * (16 * QT))
                pool.sem_inc(xq_free, 1)

            pool.wait_ge(w_split, 2)
            nc.gpsimd.tensor_tensor(w_lo[:, 2:PAIRS, :], w_f[:, 2:PAIRS, :], w_hi[:, 2:PAIRS, :].bitcast(F32),
                                    ALU.subtract).then_inc(w_split, 1)
            for k in range(LEAD):
                body(None, k, first=k == 0)
            with pool.Fori(0, ROUNDS) as i:
                steps.restart()
                for k in range(LEAD, LEAD + PAIRS):
                    body(i, k)
            steps.restart()
            for k in range(GROUPS - LEAD, GROUPS):
                body(None, k)
            scatter(BATCHES)
            first = 0
            for part in range(2):
                stored = A_TILES if part == 0 else SLOT_TILES
                for m in range(3):
                    pool.wait_ge(y_stored[m], 16 * len(range(m, stored, 3)))
                pool.wait_ge(rows_known, part + 1)
                for t in range(first, first + PART_TOKEN_TILES[part]):
                    nc.gpsimd.indirect_dma_start(
                        out=yr[:, t, :], out_offset=None, in_=sorted_ys[part],
                        in_offset=bass.IndirectOffsetOnAxis(ap=row[:, t:t + 1], axis=0)).then_inc(gathered[t // QT], 16)
                first += PART_TOKEN_TILES[part]

        @block.scalar
        def _(act):
            def squares(i, k, bank=6, first=False):
                act.wait_ge(qk_projected, total(i, k, 1, 1))
                if not first:
                    act.wait_ge(squares_summed, total(i, k, 1, 0))
                nc.scalar.activation(sq[:].rearrange("p a b -> p (a b)"),
                                     ps[:, bank:bank + 2, :].rearrange("p a b -> p (a b)"), ACT.Square).then_inc(squared, 1)

            def copy_v(g, half, copies):
                act.wait_ge(v_projected, copies)
                nc.scalar.activation(v[:, g % 4:g % 4 + 2, 2 * half:2 * half + 2, :].rearrange("p g t d -> p t g d"),
                                     DEN.rearrange("p (t g d) -> p t g d", t=2, g=2), ACT.Copy).then_inc(v_copied, 1)

            def tanh(i, k, j):
                act.wait_ge(scored, total(i, k, 4, j + 1))
                nc.scalar.activation(pr[:, k % 2, j, :], S[j % 2].rearrange("p a b -> p (a b)"), ACT.Tanh,
                                     scale=1.0 / CLAMP).then_inc(tanh_done, 1)

            def exps(i, k, half):
                act.wait_ge(tanh_done, total(i, k, 4, 2 * half + 2))
                w = pr[:, k % 2, 2 * half:2 * half + 2, :].rearrange("p a b -> p (a b)")
                nc.scalar.activation(w, w, ACT.Exp, scale=CLAMP / DH ** 0.5).then_inc(exp_done, 1)

            def high(dst, src, scale, done):
                nc.scalar.activation(dst, src, ACT.Copy, scale=scale).then_inc(done, 1)

            def high_q(i, k):
                act.wait_ge(q_transposed, total(i, k, 1, 1))
                high(qt_hi[:, k % 2, :], XB, scale_qk[:, 0, k % PAIRS:k % PAIRS + 1], qt_hi_ready)

            def high_k(i, k):
                act.wait_ge(k_transposed, total(i, k, 1, 1))
                high(kt_hi[:, k % 2, :], XA, scale_qk[:, 1, k % PAIRS:k % PAIRS + 1], kt_hi_ready)

            def high_xt(n):
                act.wait_ge(xt_transposed, n)
                high(xt_hi[:], DEN, norm_col[:, 0:1], xt_hi_ready)

            def router_steps(c, n):
                if c == 1:
                    act.wait_ge(xq_transposed, n)
                    high(xrt[:], DEN, rms_col[:, 0:1], xrt_ready)
                if c == 2:
                    act.wait_ge(logits_done, n)
                    high(batch_logits[:].rearrange("p a b -> p (a b)"), DEN[:, 0:QT * EXPERTS], 1.0, logits_copied)
                if c == 3:
                    act.wait_ge(ranked, n)
                    high(ranks[:].rearrange("p a e t -> p (a e t)"), DEN[:, 0:2 * QT * EXPERTS], 1.0, ranks_copied)

            def body(i, k, first=False, prepare=True, score_next=True):
                c, done = k % PAIRS, k >= PAIRS
                if score_next:
                    if not first:
                        act.wait_ge(pv_done, total(i, k, 1, 0))
                        act.wait_ge(sums_ready, total(i, k, 1, 0))
                    tanh(i, k + 1, 0)
                if prepare:
                    squares(i, k + 2)
                if score_next:
                    tanh(i, k + 1, 1)
                if done and c in (2, 3):
                    router_steps(c, batch(i, k))
                if score_next:
                    exps(i, k + 1, 0)
                    tanh(i, k + 1, 2)
                if prepare:
                    copy_v(k + 2 - k % 2, k % 2, total(i, k, 1, 3))
                    high_q(i, k + 2)
                    high_k(i, k + 2)
                if c == 5 and k < GROUPS - LEAD:
                    high_xt(batch(i, k, 2))
                if done and c == 1:
                    router_steps(c, batch(i, k))
                if score_next:
                    tanh(i, k + 1, 3)
                if score_next:
                    exps(i, k + 1, 1)

            act.wait_ge(made, 2)
            nc.scalar.activation(warm[:], ones[:, 0:1], ACT.Tanh)
            act.wait_ge(w_first_loaded, 48)
            high(w_hi[:, 0:2, :], w_f[:, 0:2, :], 1.0, w_split)
            act.wait_ge(cols_loaded, 64)
            high_xt(1)
            act.wait_ge(w_loaded, 48)
            high(w_hi[:, 2:PAIRS, :], w_f[:, 2:PAIRS, :], 1.0, w_split)
            act.wait_ge(scale_ready, 1)
            squares(None, 0, first=True)
            squares(None, 1, bank=2)
            high_q(None, 0)
            high_k(None, 0)
            tanh(None, 0, 0)
            high_q(None, 1)
            high_k(None, 1)
            tanh(None, 0, 1)
            copy_v(0, 0, 1)
            exps(None, 0, 0)
            tanh(None, 0, 2)
            copy_v(0, 1, 2)
            tanh(None, 0, 3)
            exps(None, 0, 1)
            act.wait_ge(w_split, 3)
            for k in range(LEAD):
                body(None, k, first=k == 0)
            with act.Fori(0, ROUNDS) as i:
                for k in range(LEAD, LEAD + PAIRS):
                    body(i, k)
            for k in range(GROUPS - LEAD, GROUPS):
                body(None, k, prepare=k + 2 < GROUPS, score_next=k + 1 < GROUPS)

            def move_xst(s, m):
                act.wait_ge(xs_transposed, s + 1)
                high(xst[m % 3], XST, rms_col[:, 0:1], xst_ready)

            def tanh_pre(s, m):
                act.wait_ge(pre_ready, s + 1)
                nc.scalar.activation(th[m % 3], pre[m % 3], ACT.Tanh, scale=0.5).then_inc(th_ready, 1)

            def store(s, m, part):
                act.wait_ge(y_ready, s + 1)
                act.dma_start(sorted_ys[part][bass.ds((s - part * A_TILES) * P, P), :], ys[m % 3]).then_inc(y_stored[m % 3], 16)

            def tile(s, m, first=False, ahead2=True, ahead3=True, part=0):
                act.wait_ge(h_transposed, s + 1)
                if not first:
                    act.wait_ge(down_done, s)
                nc.scalar.activation(ht_sb, HT, ACT.Copy, scale=0.5).then_inc(ht_copied, 1)
                if ahead3:
                    move_xst(s + 3, m + 3)
                if ahead2:
                    tanh_pre(s + 2, m + 2)
                if not first:
                    store(s - 1, m + 2, part)

            for s in range(3):
                move_xst(s, s)
            act.wait_ge(pv_done, GROUPS)
            act.wait_ge(sums_ready, GROUPS)
            tanh_pre(0, 0)
            tanh_pre(1, 1)
            for s in range(LEAD_TILES):
                tile(s, s, first=s == 0)
                if s in (8, 9, 11):
                    router_steps({8: 1, 9: 2, 11: 3}[s], BATCHES)
                if s == 11:
                    act.wait_ge(shifted_ready, 1)
                    nc.scalar.activation(rb, ra, ACT.Exp).then_inc(score_exp_done, 1)
            with act.Fori(0, LOOP_ROUNDS) as i:
                for k in range(ROUND_TILES):
                    tile(i * ROUND_TILES + (LEAD_TILES + k), k)
            for s in REST_TILES:
                tile(s, s, ahead2=s + 2 < SLOT_TILES, ahead3=s + 3 < SLOT_TILES, part=int(s > A_TILES))
            store(SLOT_TILES - 1, SLOT_TILES - 1, 1)

            for n, tiles in enumerate(NORM_CHUNKS[:-1]):
                act.wait_ge(norm_ready, n + 1)
                for t in tiles:
                    last = nc.scalar.activation(yr[:, t, :], yr[:, t, :], ACT.Identity, bias=ss[:, t:t + 1],
                                                scale=rs[:, t:t + 1])
                    if (t + 1) % QT == 0:
                        last.then_inc(out_ready, 1)

        @block.vector
        def _(dve):
            V = nc.vector
            steps = Steps(dve, dve_steps)

            def rsqrt(cols):
                y, s, a, b = rs[:, cols], ss[:, cols], na[:, cols], nb[:, cols]
                steps.after(V.tensor_scalar(y.bitcast(I32), s.bitcast(I32), -0.5, RSQRT_MAGIC, ALU.mult, ALU.add))
                steps.after(V.tensor_tensor(a, y, s, ALU.mult))
                steps.after(V.tensor_tensor(b, a, y, ALU.mult))
                steps.after(V.scalar_tensor_tensor(a, b, -10.0 / 3.0, b, ALU.add, ALU.mult))
                steps.after(V.scalar_tensor_tensor(y, a, 5.0, y, ALU.add, ALU.mult))
                steps.after(V.scalar_tensor_tensor(a, y, -0.5 * 0.375 ** 3, s, ALU.mult, ALU.mult))
                steps.after(V.tensor_tensor(b, a, y, ALU.mult))
                steps.after(V.scalar_tensor_tensor(y, b, 1.5 * 0.375, y, ALU.add, ALU.mult))

            HEAD_COLS = slice(0, 16)
            ROW_COLS = slice(16, 16 + QT)

            def rows_squares(rows, eps):
                tmp = den_t[:].rearrange("p (a b) -> p a b", b=D)
                steps.after(V.tensor_tensor(tmp, rows, rows, ALU.mult))
                steps.after(V.tensor_reduce(ss[:, ROW_COLS], tmp, AX_X, ALU.add))
                steps.after(V.tensor_scalar(ss[:, ROW_COLS], ss[:, ROW_COLS], 1.0 / D, eps, ALU.mult, ALU.add))

            def centre(rows):
                steps.after(V.tensor_reduce(ss[:, ROW_COLS], rows, AX_X, ALU.add))
                steps.after(V.tensor_scalar(ss[:, ROW_COLS], ss[:, ROW_COLS], 1.0 / D, None, ALU.mult))
                steps.after(V.tensor_tensor(rows, rows, ss[:, ROW_COLS].unsqueeze(2).to_broadcast([P, QT, D]), ALU.subtract))

            def head_norms(i, k):
                dve.wait_ge(squared, total(i, k, 1, 1))
                V.tensor_reduce(ss[:, HEAD_COLS], sq[:].rearrange("p a (h d) -> p (a h) d", d=DH), AX_X,
                                ALU.add).then_inc(squares_summed, 1)
                dve.wait_ge(squares_summed, total(i, k, 1, 1))
                steps.after(V.tensor_scalar(ss[:, HEAD_COLS], ss[:, HEAD_COLS], TINY, None, ALU.max))
                rsqrt(HEAD_COLS)

            def scale_heads(i, k, banks=(XA, XB), first=False):
                if not first:
                    dve.wait_ge(k_transposed, total(i, k, 1, 0))
                for half, bank in enumerate(banks):
                    V.tensor_tensor(qk[:, 2 * half:2 * half + 2, :].rearrange("p a (h d) -> p (a h) d", d=DH),
                                    bank.rearrange("p (a d) -> p a d", d=DH),
                                    rs[:, 8 * half:8 * half + 8].unsqueeze(2).to_broadcast([P, 8, DH]),
                                    ALU.mult).then_inc(qk_scaled, 1)

            def low(dst, src, scale, hi, done):
                V.scalar_tensor_tensor(dst, src, scale, hi.bitcast(F32), ALU.mult, ALU.subtract).then_inc(done, 1)

            def low_q(i, k):
                dve.wait_ge(qt_hi_ready, total(i, k, 1, 1))
                low(qt_lo[:, k % 2, :], XB, scale_qk[:, 0, k % PAIRS:k % PAIRS + 1], qt_hi[:, k % 2, :], qt_ready)

            def low_k(i, k):
                dve.wait_ge(kt_hi_ready, total(i, k, 1, 1))
                low(kt_lo[:, k % 2, :], XA, scale_qk[:, 1, k % PAIRS:k % PAIRS + 1], kt_hi[:, k % 2, :], kt_ready)

            def low_xt(n):
                dve.wait_ge(xt_hi_ready, n)
                low(xt_lo[:], DEN, norm_col[:, 0:1], xt_hi[:], xt_ready)

            def normalise(i, k):
                dve.wait_ge(den_done, total(i, k, 1, 1))
                steps.after(V.transpose(den_t[:], DEN))
                steps.after(V.reciprocal(den_r[:], den_t[:].rearrange("p (a b) -> p a b", b=32)[:, :, 0]))
                steps.after(V.transpose(den_t[:].rearrange("p (a b) -> p a b", b=32),
                                        den_r[:].unsqueeze(2).to_broadcast([P, SEQ // 32, 32])))
                V.tensor_tensor(at[:, k % PAIRS, :], AV, den_t[:], ALU.mult).then_inc(at_ready, 1)
                dve.wait_ge(at_ready, total(i, k, 1, 1))

            def x_squares(b):
                rows_squares(x[:, bass.ds(b * QT, QT), :], EPS_ATTN)

            def x_hat(b):
                rows = x[:, bass.ds(b * QT, QT), :]
                V.tensor_tensor(xh[:], rows, rs[:, ROW_COLS].unsqueeze(2).to_broadcast([P, QT, D]),
                                ALU.mult).then_inc(xh_ready, 1)

            def residual(b, n, transposed):
                dve.wait_ge(xt_transposed, transposed)
                dve.wait_ge(wo_done, n)
                V.tensor_tensor(xh[:].rearrange("p a b -> p (a b)"),
                                x[:, bass.ds(b * QT, QT), :].rearrange("p a b -> p (a b)"), DEN,
                                ALU.add).then_inc(x1_ready, 1)

            def layer_norm_1(b):
                steps.after(V.tensor_tensor(x[:, bass.ds(b * QT, QT), :], xh[:],
                                            rs[:, ROW_COLS].unsqueeze(2).to_broadcast([P, QT, D]), ALU.mult))

            def router_squares(b):
                rows_squares(x[:, bass.ds(b * QT, QT), :], EPS_FFN)

            def router_rows(b, n):
                dve.wait_ge(xq_free, n)
                rows = x[:, bass.ds(b * QT, QT), :]
                V.tensor_tensor(xq[:], rows, rs[:, ROW_COLS].unsqueeze(2).to_broadcast([P, QT, D]),
                                ALU.mult).then_inc(xq_ready, 1)

            def choose(b, n):
                dve.wait_ge(logits_copied, n)
                lg, tp = logits[:, bass.ds(b * QT, QT), :], top[:, bass.ds(b * QT, QT)]
                steps.after(V.tensor_reduce(least[:], batch_logits[:], AX_X, ALU.max))
                V.tensor_copy(lg, batch_logits[:])
                V.tensor_copy(tp, least[:])
                steps.after(V.tensor_tensor(is_top[:], batch_logits[:], least[:].unsqueeze(2).to_broadcast([P, QT, EXPERTS]),
                                            ALU.is_equal))
                steps.after(V.scalar_tensor_tensor(
                    choice[:], is_top[:], -float(EXPERTS),
                    count[:, 0:EXPERTS].unsqueeze(1).to_broadcast([P, QT, EXPERTS]), ALU.mult, ALU.add))
                steps.after(V.tensor_reduce(least[:], choice[:], AX_X, ALU.min))
                V.tensor_tensor(hot[:].rearrange("p e t -> p t e"), choice[:],
                                least[:].unsqueeze(2).to_broadcast([P, QT, EXPERTS]), ALU.is_equal).then_inc(hot_ready, 1)

            def assign(b, n):
                flat = lambda a: a.rearrange("p e t -> p (e t)")
                dve.wait_ge(next_slot_ready, n)
                dve.wait_ge(ranks_copied, n)
                steps.after(V.tensor_tensor_scan(flat(incl[:]), flat(carry[:]), flat(tot), 0.0, ALU.mult, ALU.add))
                steps.after(V.tensor_tensor(rank[:], ranks[:, 0, :, :], incl[:], ALU.add))
                steps.after(V.tensor_tensor(rank[:], rank[:], tot, ALU.subtract))
                steps.after(V.tensor_tensor(rank[:], rank[:], next_slot[:].unsqueeze(2).to_broadcast([P, EXPERTS, QT]),
                                            ALU.add))
                steps.after(V.tensor_tensor(rank[:], rank[:], hot[:], ALU.mult))
                steps.after(V.tensor_reduce(slot_f[:], rank[:].rearrange("p e t -> p t e"), AX_X, ALU.add))
                steps.after(V.tensor_copy(slot[:, bass.ds(b * QT, QT)], slot_f[:]))
                V.tensor_copy(batch_slot[:], slot_f[:]).then_inc(slots_ready, 1)

            def body(i, k, prepare=True):
                c, done = k % PAIRS, k >= PAIRS
                n = batch(i, k)
                ahead = k < GROUPS - LEAD
                if prepare:
                    head_norms(i, k + 2)
                    scale_heads(i, k + 2)
                if c == 0 and done:
                    residual(batch(i, k, -1), n, batch(i, k, 1))
                    dve.wait_ge(x1_ready, n)
                    centre(xh[:])
                    rows_squares(xh[:], EPS_LN)
                    rsqrt(ROW_COLS)
                if c == 1 and done:
                    rsqrt(ROW_COLS)
                    router_rows(batch(i, k, -1), n)
                if c == 2 and done:
                    choose(batch(i, k, -1), n)
                if c == 3 and done:
                    assign(batch(i, k, -1), n)
                if c == 4 and ahead:
                    x_squares(batch(i, k, 1))
                if c == 5 and ahead:
                    x_hat(batch(i, k, 1))
                if prepare:
                    low_q(i, k + 2)
                    low_k(i, k + 2)
                if c == 0 and done:
                    layer_norm_1(batch(i, k, -1))
                    router_squares(batch(i, k, -1))
                if c == 4 and ahead:
                    rsqrt(ROW_COLS)
                if c == 5 and ahead:
                    low_xt(batch(i, k, 2))
                normalise(i, k)

            dve.wait_ge(x0_loaded, 16)
            x_squares(0)
            rsqrt(ROW_COLS)
            x_hat(0)
            dve.wait_ge(cols_loaded, 64)
            V.tensor_scalar(scale_qk[:], gam[:], 1.0, DH ** 0.5, ALU.add, ALU.mult).then_inc(scale_ready, 1)
            dve.wait_ge(w_split, 1)
            V.tensor_tensor(w_lo[:, 0:2, :], w_f[:, 0:2, :], w_hi[:, 0:2, :].bitcast(F32), ALU.subtract).then_inc(w_first_split, 1)
            low_xt(1)
            V.memset(carry[:], 1.0).then_inc(scale_ready, 1)
            dve.wait_ge(scale_ready, 2)
            V.memset(carry[:, :, 0:1], 0.0)
            dve.wait_ge(made, 3)
            steps.after(V.tensor_copy(count[:], count_i[:]))
            V.tensor_scalar(tile_starts[:], count[:, 0:TILES], float(P), None, ALU.mult)
            for part, tiles in enumerate(PART_TOKEN_TILES):
                V.tensor_scalar(first_slots[:, part, :], count[:, 0:EXPERTS], float(tiles * P),
                                float(part * PART_DRAM_TILES[0] * P), ALU.mult, ALU.add)
            V.tensor_scalar(next_slot[:], count[:, 0:EXPERTS], float(PART_TOKEN_TILES[0] * P), None,
                            ALU.mult).then_inc(next_slot_ready, 1)
            dve.sem_inc(xq_free, 1)
            head_norms(None, 0)
            scale_heads(None, 0, first=True)
            head_norms(None, 1)
            low_q(None, 0)
            low_k(None, 0)
            scale_heads(None, 1, banks=(ps[:, 2, :], ps[:, 3, :]))
            low_q(None, 1)
            low_k(None, 1)
            dve.wait_ge(x_loaded, 16)
            for k in range(LEAD):
                body(None, k)
            with dve.Fori(0, ROUNDS) as i:
                steps.restart()
                for k in range(LEAD, LEAD + PAIRS):
                    body(i, k)
            steps.restart()
            def count_tiles(part):
                per_expert = PART_TOKEN_TILES[part]
                firsts = first_slots[:, part, :]
                starts = ra[:, 0:EXPERTS * per_expert].rearrange("p (e t) -> p e t", e=EXPERTS)
                below = [P, EXPERTS, per_expert]
                dve.wait_ge(next_slot_ready, BATCHES + part)
                steps.after(V.tensor_tensor(n_tiles[:], next_slot[:], firsts, ALU.subtract))
                if part == 0:
                    V.tensor_copy(next_slot[:], first_slots[:, 1, :])
                steps.after(V.tensor_tensor(starts, n_tiles[:].unsqueeze(2).to_broadcast(below),
                                            tile_starts[:, 0:per_expert].unsqueeze(1).to_broadcast(below), ALU.is_gt))
                steps.after(V.tensor_reduce(n_tiles[:], starts, AX_X, ALU.add))
                steps.after(V.tensor_tensor_scan(ends[:], ones[:, 0:EXPERTS], n_tiles[:], 0.0, ALU.mult, ALU.add))

            def slot_tiles(part):
                per_expert, n_slot = PART_TOKEN_TILES[part], PART_SLOT_TILES[part]
                s0 = part * A_TILES
                base = part * PART_DRAM_TILES[0]
                numbers = count[:, 0:n_slot]
                all_s = [P, n_slot, EXPERTS]
                past = cmp_s[:, 0:n_slot * EXPERTS].rearrange("p (s e) -> p s e", e=EXPERTS)
                left = cmp_n[:, 0:n_slot * EXPERTS].rearrange("p (s e) -> p s e", e=EXPERTS)
                steps.after(V.tensor_tensor(past, numbers.unsqueeze(2).to_broadcast(all_s),
                                            ends[:].unsqueeze(1).to_broadcast(all_s), ALU.is_ge))
                steps.after(V.tensor_reduce(owner_f[:, 0:n_slot], past, AX_X, ALU.add))
                steps.after(V.tensor_scalar(n_tiles[:], n_tiles[:], -1.0, float(per_expert), ALU.mult, ALU.add))
                steps.after(V.tensor_tensor(left, past, n_tiles[:].unsqueeze(1).to_broadcast(all_s), ALU.mult))
                steps.after(V.tensor_reduce(place_f[:, 0:n_slot], left, AX_X, ALU.add))
                steps.after(V.tensor_scalar(place_f[:, 0:n_slot], place_f[:, 0:n_slot], 1.0, float(base), ALU.mult, ALU.add))
                steps.after(V.tensor_tensor(place[:, s0:s0 + n_slot], place_f[:, 0:n_slot], numbers, ALU.add))
                V.tensor_scalar(owner[:, s0:s0 + n_slot], owner_f[:, 0:n_slot], float(EXPERTS - 1), None,
                                ALU.min).then_inc(owners_ready, 1)
                dve.wait_ge(owners_ready, part + 1)

            def token_rows(part):
                per_expert, t0 = PART_TOKEN_TILES[part], part * PART_TOKEN_TILES[0]
                base = part * PART_DRAM_TILES[0]
                firsts = first_slots[:, part, :]
                tokens_ = slice(t0, t0 + per_expert)
                te7 = lambda a: a[:, 0:per_expert * (EXPERTS - 1)].rearrange("p (t e) -> p t e", e=EXPERTS - 1)
                by_token = [P, per_expert, EXPERTS - 1]
                steps.after(V.tensor_tensor(te7(ra), slot[:, tokens_].unsqueeze(2).to_broadcast(by_token),
                                            firsts[:, 1:EXPERTS].unsqueeze(1).to_broadcast(by_token), ALU.is_ge))
                steps.after(V.tensor_tensor(te7(rb), te7(ra), n_tiles[:, 0:EXPERTS - 1].unsqueeze(1).to_broadcast(by_token),
                                            ALU.mult))
                steps.after(V.tensor_reduce(row_f[:, tokens_], te7(rb), AX_X, ALU.add))
                steps.after(V.tensor_scalar(row_f[:, tokens_], row_f[:, tokens_], -float(P), -float(base * P),
                                            ALU.mult, ALU.add))
                V.tensor_tensor(row[:, tokens_], row_f[:, tokens_], slot[:, tokens_], ALU.add).then_inc(rows_known, 1)
                dve.wait_ge(rows_known, part + 1)

            for k in range(GROUPS - LEAD, GROUPS):
                body(None, k, prepare=k + 2 < GROUPS)
                if k == GROUPS - 3:
                    count_tiles(0)
                    slot_tiles(0)
                    token_rows(0)
            dve.wait_ge(ffn_loaded, 64)

            DVE = mybir.EngineType.DVE

            def hidden_pre(s, m, e):
                dve.wait_ge(up_done, s + 1)
                V.tensor_tensor(pre[m % 3], U[m % 3], b_1[:, bass.ds(e, 1), :].rearrange("p a b -> p (a b)"),
                                ALU.add).then_inc(pre_ready, 1)

            def hidden(s, m):
                dve.wait_ge(th_ready, s + 1)
                V.scalar_tensor_tensor(hid[m % 3], th[m % 3], 1.0, pre[m % 3], ALU.add, ALU.mult).then_inc(hid_ready, 1)

            def tile_out(s, m, e, stored=None):
                dve.wait_ge(down_done, s + 1)
                if stored is not None:
                    dve.wait_ge(y_stored[m % 3], stored)
                V.tensor_tensor(ys[m % 3], Y, b_2[:, bass.ds(e, 1), :].rearrange("p a b -> p (a b)"),
                                ALU.add).then_inc(y_ready, 1)

            def tile(s, k, known, stored=None, before=True, ahead1=True, ahead2=True, ahead3=True):
                if before:
                    tile_out(s - 1, k + 2, known[k - 1], stored)
                if ahead1:
                    hidden(s + 1, k + 1)
                if ahead3:
                    known[k + 3], = experts(DVE, s + 3, 1)
                if ahead2:
                    hidden_pre(s + 2, k + 2, known[k + 2])

            def router_softmax():
                te = lambda a: a.rearrange("p (t e) -> p t e", e=EXPERTS)
                V.tensor_tensor(te(ra), logits[:], top[:].unsqueeze(2).to_broadcast([P, TILES, EXPERTS]),
                                ALU.subtract).then_inc(shifted_ready, 1)

            def top_score():
                dve.wait_ge(score_exp_done, 1)
                steps.after(V.tensor_reduce(score[:], rb.rearrange("p (t e) -> p t e", e=EXPERTS), AX_X, ALU.add))
                steps.after(V.reciprocal(score[:], score[:]))

            def row_stats(b):
                tiles = range(b * QT, (b + 1) * QT)
                dve.wait_ge(gathered[b], 16 * QT)
                for t in tiles:
                    last = V.scalar_tensor_tensor(yr[:, t, :], yr[:, t, :], score[:, t:t + 1], x[:, t, :], ALU.mult, ALU.add)
                steps.after(last)
                for t in tiles:
                    last = V.bn_stats(stats[:, t - tiles.start, :], yr[:, t, :])
                steps.after(last)
                for t in tiles:
                    last = V.bn_aggr(mv[:, t, :], stats[:, t - tiles.start, :])
                steps.after(last)

            known = dict(enumerate(experts(DVE, 0, 3)))
            hidden_pre(0, 0, known[0])
            hidden(0, 0)
            hidden_pre(1, 1, known[1])
            last = BATCHES - 1
            residual(last, BATCHES, BATCHES)
            dve.wait_ge(x1_ready, BATCHES)
            for s in range(LEAD_TILES):
                if s == 1:
                    centre(xh[:])
                if s == 2:
                    rows_squares(xh[:], EPS_LN)
                if s in (3, 6):
                    rsqrt(ROW_COLS)
                if s == 4:
                    layer_norm_1(last)
                if s == 5:
                    router_squares(last)
                if s == 7:
                    router_rows(last, BATCHES)
                if s == 10:
                    choose(last, BATCHES)
                if s == 11:
                    router_softmax()
                if s == 12:
                    top_score()
                if s == 13:
                    assign(last, BATCHES)
                if s == 14:
                    count_tiles(1)
                tile(s, s, known, stored=16 * ((s - 1) // 3) if s >= 4 else None, before=s >= 1)
            slot_tiles(1)
            with dve.Fori(0, LOOP_ROUNDS) as i:
                s0 = i * ROUND_TILES + LEAD_TILES
                known = dict(zip(range(-1, 3), experts(DVE, s0 - 1, 4)))
                for k in range(ROUND_TILES):
                    tile(s0 + k, k, known, stored=i * (16 * ROUND_TILES // 3) + 16 * ((LEAD_TILES + k - 1) // 3),
                         ahead3=k + 1 < ROUND_TILES)
            s0 = REST_TILES.start
            known = dict(zip(range(s0 - 1, s0 + 3), experts(DVE, s0 - 1, 4)))
            early = {39: 0, 41: 1, 43: 2, 45: 3}
            for s in REST_TILES:
                if s == A_TILES + 1:
                    token_rows(1)
                tile(s, s, known, stored=16 * ((s - 1) // 3), ahead1=s + 1 < SLOT_TILES, ahead2=s + 2 < SLOT_TILES,
                     ahead3=s + 3 < SLOT_TILES)
                if s in early:
                    row_stats(early[s])
            tile_out(SLOT_TILES - 1, SLOT_TILES - 1, known[SLOT_TILES - 1], stored=16 * ((SLOT_TILES - 1) // 3))

            for n, tiles in enumerate(NORM_CHUNKS):
                w = slice(tiles.start, tiles.stop)
                for b in range(tiles.start // QT, tiles.stop // QT):
                    if b not in early.values():
                        row_stats(b)
                steps.after(V.tensor_scalar(ss[:, w], mv[:, w, 1], 1.0, EPS_LN, ALU.mult, ALU.add))
                rsqrt(w)
                if n < len(NORM_CHUNKS) - 1:
                    V.scalar_tensor_tensor(ss[:, w], mv[:, w, 0], -1.0, rs[:, w], ALU.mult, ALU.mult).then_inc(norm_ready, 1)
                    dve.wait_ge(norm_ready, n + 1)
            for t in NORM_CHUNKS[-1]:
                last = V.tensor_scalar(yr[:, t, :], yr[:, t, :], mv[:, t, 0:1], rs[:, t:t + 1], ALU.subtract, ALU.mult)
            last.then_inc(last_out_ready, 1)

        @block.tensor
        def _(pe):
            mm = nc.tensor.matmul

            def split_mm(out_, lhs_hi, lhs_lo, rhs_hi, rhs_lo):
                mm(out_, lhs_lo, rhs_hi, start=True, stop=False)
                mm(out_, lhs_hi, rhs_lo, start=False, stop=False)
                return mm(out_, lhs_hi, rhs_hi, start=False, stop=True)

            def project_qk(i, k, b, bank=6, first=False):
                pe.wait_ge(xt_ready, b)
                if not first:
                    pe.wait_ge(kt_ready, total(i, k, 1, 0))
                    pe.wait_ge(qt_ready, total(i, k, 1, 0))
                c = k % PAIRS
                for t in range(QT):
                    rows = slice(t * P, (t + 1) * P)
                    last = split_mm(ps[:, bank + t // 2, (t % 2) * 256:(t % 2) * 256 + 256], xt_hi[:, rows], xt_lo[:, rows],
                                    w_hi[:, c, 0:2 * P], w_lo[:, c, 0:2 * P])
                last.then_inc(qk_projected, 1)

            def project_v(k, half):
                c = k % PAIRS
                for t in (0, 1):
                    rows = slice((2 * half + t) * P, (2 * half + t + 1) * P)
                    last = split_mm(DEN[:, t * 2 * P:(t + 1) * 2 * P], xt_hi[:, rows], xt_lo[:, rows],
                                    w_hi[:, c:c + 2, 2 * P:3 * P], w_lo[:, c:c + 2, 2 * P:3 * P])
                last.then_inc(v_projected, 1)

            def transpose_qk(i, k):
                pe.wait_ge(qk_scaled, total(i, k, 2, 2))
                for bank, cols, done in ((XB, slice(0, P), q_transposed), (XA, slice(P, 2 * P), k_transposed)):
                    for t in range(QT):
                        last = nc.tensor.transpose(bank[:, t * P:(t + 1) * P], qk[:, t, cols], ident[:])
                    last.then_inc(done, 1)

            def scores(i, k, j, fresh=False):
                if j == 0:
                    pe.wait_ge(qt_ready, total(i, k, 1, 1))
                    pe.wait_ge(kt_ready, total(i, k, 1, 1))
                if not fresh:
                    pe.wait_ge(tanh_done, total(i, k, 4, j - 1))
                for n, (keys_, queries) in enumerate(((kt_lo, qt_hi), (kt_hi, qt_lo), (kt_hi, qt_hi))):
                    for h in range(2):
                        rows = slice(DH * h, DH * (h + 1))
                        last = mm(S[j % 2][:, h, :], keys_[rows, k % 2, j * P:(j + 1) * P], queries[rows, k % 2, :],
                                  start=n == 0, stop=n == 2)
                last.then_inc(scored, 1)

            def pv(i, k, j, first=False):
                if j % 2 == 0:
                    pe.wait_ge(exp_done, total(i, k, 2, j // 2 + 1))
                if j == 0:
                    if first:
                        pe.wait_ge(v_copied, 2)
                    else:
                        pe.wait_ge(at_ready, total(i, k, 1, 0))
                for h in range(2):
                    last = mm(AV[DH * h:DH * (h + 1), :], v[:, k % 4, j, DH * h:DH * (h + 1)],
                              pr[:, k % 2, j, h * SEQ:(h + 1) * SEQ], start=j == 0, stop=j == QT - 1)
                if j == QT - 1:
                    last.then_inc(pv_done, 1)

            def softmax_sums(i, k):
                pe.wait_ge(sums_ready, total(i, k, 1, 1))
                for h in range(2):
                    last = mm(DEN[DH * h:DH * (h + 1), :], ones[:, 0:DH], sums[:, h * SEQ:(h + 1) * SEQ],
                              start=True, stop=True)
                last.then_inc(den_done, 1)

            def output_projection(n):
                for t in range(QT):
                    for c in range(PAIRS):
                        last = mm(DEN[:, t * D:(t + 1) * D], at[:, c, t * P:(t + 1) * P], w_o[:, c, :],
                                  start=c == 0, stop=c == PAIRS - 1)
                last.then_inc(wo_done, 1)

            def transpose_rows(rows, done):
                for t in range(QT):
                    last = nc.tensor.transpose(DEN[:, t * P:(t + 1) * P], rows[:, t, :], ident[:])
                last.then_inc(done, 1)

            def router_logits(n):
                pe.wait_ge(xrt_ready, n)
                for t in range(QT):
                    last = mm(DEN[:, t * EXPERTS:(t + 1) * EXPERTS], xrt[:, t * P:(t + 1) * P], gate_t[:],
                              start=True, stop=True)
                last.then_inc(logits_done, 1)

            def rank_tokens(n):
                pe.wait_ge(hot_ready, n)
                w, hots = QT * EXPERTS, hot[:].rearrange("p e t -> p (e t)")
                mm(DEN[:, 0:w], before[:], hots, start=True, stop=True)
                mm(DEN[:, w:2 * w], ones[:], hots, start=True, stop=True).then_inc(ranked, 1)

            def stay_warm(n):
                for _ in range(n):
                    mm(AV, ones[:], xt_hi[:].bitcast(F32), start=True, stop=True)

            def body(i, k, first=False):
                c, done = k % PAIRS, k >= PAIRS
                prepare, score_next = k + 2 < GROUPS, k + 1 < GROUPS
                n = batch(i, k)
                if score_next:
                    scores(i, k + 1, 0)
                if prepare:
                    project_qk(i, k + 2, batch(i, k + 2, 1))
                if score_next:
                    scores(i, k + 1, 1)
                pv(i, k, 0, first)
                if c == 0 and done:
                    output_projection(n)
                if c == 2 and done:
                    router_logits(n)
                if c == 3 and done:
                    rank_tokens(n)
                pv(i, k, 1)
                if score_next:
                    scores(i, k + 1, 2)
                pv(i, k, 2)
                if done and c in (0, 2, 3):
                    pe.wait_ge({0: x1_ready, 2: logits_copied, 3: ranks_copied}[c], n)
                if prepare:
                    project_v(k + 2 - k % 2, k % 2)
                    transpose_qk(i, k + 2)
                if c == 5 and k < GROUPS - LEAD:
                    pe.wait_ge(v_copied, total(i, k, 1, 3))
                    pe.wait_ge(xh_ready, batch(i, k, 2))
                    transpose_rows(xh, xt_transposed)
                if score_next:
                    scores(i, k + 1, 3)
                if prepare:
                    pe.wait_ge(v_copied, total(i, k, 1, 3))
                if c == 1 and done:
                    pe.wait_ge(xq_ready, n)
                    transpose_rows(xq, xq_transposed)
                pv(i, k, 3)
                if c == 1 and done:
                    pe.wait_ge(xrt_ready, n)
                if c == 5 and k < GROUPS - LEAD:
                    pe.wait_ge(xt_ready, batch(i, k, 2))
                softmax_sums(i, k)

            pe.wait_ge(consts_ready, 2)
            pe.wait_ge(xh_ready, 1)
            transpose_rows(xh, xt_transposed)
            pe.wait_ge(w_first_split, 1)
            project_qk(None, 0, 1, first=True)
            project_qk(None, 1, 1, bank=2, first=True)
            stay_warm(5)
            transpose_qk(None, 0)
            stay_warm(3)
            scores(None, 0, 0, fresh=True)
            transpose_qk(None, 1)
            scores(None, 0, 1, fresh=True)
            project_v(0, 0)
            scores(None, 0, 2)
            pe.wait_ge(v_copied, 1)
            project_v(0, 1)
            scores(None, 0, 3)
            pe.wait_ge(w_split, 3)
            pe.wait_ge(wo_loaded, 32)
            for k in range(LEAD):
                body(None, k, first=k == 0)
            with pe.Fori(0, ROUNDS) as i:
                for k in range(LEAD, LEAD + PAIRS):
                    body(i, k)
            for k in range(GROUPS - LEAD, GROUPS):
                body(None, k)

            PE = mybir.EngineType.PE

            def transpose_x(m, loaded):
                pe.wait_ge(xs_loaded[m % 3], loaded)
                nc.tensor.transpose(XST, xs[m % 3], ident[:]).then_inc(xs_transposed, 1)

            def up(s, m, e, fresh=False):
                pe.wait_ge(xst_ready, s + 1)
                if not fresh:
                    pe.wait_ge(pre_ready, s - 2)
                mm(U[m % 3], xst[m % 3], w_1[:, bass.ds(e, 1), :].rearrange("p a b -> p (a b)"),
                   start=True, stop=True).then_inc(up_done, 1)

            def tile(s, k, known, loaded=None, first=False, ahead2=True, ahead3=True):
                m = k % 3
                pe.wait_ge(hid_ready, s + 1)
                if not first:
                    pe.wait_ge(ht_copied, s)
                for f in range(FK):
                    last = nc.tensor.transpose(HT[:, f * P:(f + 1) * P], hid[m][:, f * P:(f + 1) * P], ident[:])
                last.then_inc(h_transposed, 1)
                if ahead2:
                    up(s + 2, m + 2, known[k + 2], fresh=first)
                if loaded is not None:
                    pe.wait_ge(xst_ready, s + 3)
                    transpose_x(m + 3, loaded)
                if ahead3:
                    known[k + 3], = experts(PE, s + 3, 1)
                pe.wait_ge(ht_copied, s + 1)
                if not first:
                    pe.wait_ge(y_ready, s)
                for f in range(FK):
                    last = mm(Y, ht_sb[:, f * P:(f + 1) * P],
                              w_2[:, bass.ds(known[k], 1), f * D:(f + 1) * D].rearrange("p a b -> p (a b)"),
                              start=f == 0, stop=f == FK - 1)
                last.then_inc(down_done, 1)

            pe.wait_ge(owners_ready, 1)
            pe.wait_ge(ffn_loaded, 64)
            for s in range(3):
                if s:
                    pe.wait_ge(xst_ready, s)
                transpose_x(s, 16)
            known = dict(enumerate(experts(PE, 0, 3)))
            up(0, 0, known[0], fresh=True)
            up(1, 1, known[1], fresh=True)
            pe.wait_ge(at_ready, GROUPS)
            output_projection(BATCHES)
            for s in range(LEAD_TILES):
                if s == 8:
                    pe.wait_ge(xq_ready, BATCHES)
                    transpose_rows(xq, xq_transposed)
                if s == 9:
                    router_logits(BATCHES)
                if s == 11:
                    rank_tokens(BATCHES)
                tile(s, s, known, loaded=16 * (s // 3) + 32, first=s == 0)
            with pe.Fori(0, LOOP_ROUNDS) as i:
                s0 = i * ROUND_TILES + LEAD_TILES
                known = dict(enumerate(experts(PE, s0, 3)))
                for k in range(ROUND_TILES):
                    tile(s0 + k, k, known, loaded=i * (16 * ROUND_TILES // 3) + (16 * ((LEAD_TILES + k) // 3) + 32),
                         ahead3=k + 1 < ROUND_TILES)
            s0 = REST_TILES.start
            known = dict(zip(range(s0, s0 + 3), experts(PE, s0, 3)))
            for s in REST_TILES:
                ahead = s + 3 < SLOT_TILES
                tile(s, s, known, loaded=16 * (s // 3) + 32 if ahead else None, ahead2=s + 2 < SLOT_TILES, ahead3=ahead)


_ORDER = ["tokens", "norm_w", "wq", "wkv", "wo", "q_gamma", "k_gamma", "rms_w", "gate_w", "w1", "b1", "w2", "b2"]


def kernel(L0_attn_tokens, L0_attn_norm_w, L0_attn_Wq, L0_attn_Wkv, L0_attn_Wo, L0_attn_q_gamma,
           L0_attn_k_gamma, L0_ffn_rms_w, L0_ffn_gate_w, L0_ffn_W1, L0_ffn_b1, L0_ffn_W2, L0_ffn_b2):
    import numpy as np
    import concourse.bacc as bacc
    from concourse.bass_utils import run_bass_kernel_spmd

    def column(a):
        return np.ascontiguousarray(np.asarray(a).reshape(-1, P).T)

    arrays = dict(
        tokens=np.asarray(L0_attn_tokens).reshape(TOKENS, D),
        norm_w=column(L0_attn_norm_w), wq=np.asarray(L0_attn_Wq), wkv=np.asarray(L0_attn_Wkv),
        wo=np.asarray(L0_attn_Wo), q_gamma=column(L0_attn_q_gamma), k_gamma=column(L0_attn_k_gamma),
        rms_w=column(L0_ffn_rms_w), gate_w=np.ascontiguousarray(np.asarray(L0_ffn_gate_w).T),
        w1=np.asarray(L0_ffn_W1), b1=np.asarray(L0_ffn_b1).reshape(1, -1),
        w2=np.asarray(L0_ffn_W2), b2=np.asarray(L0_ffn_b2).reshape(1, -1),
    )
    nc = bacc.Bacc("TRN2", target_bir_lowering=False, num_devices=1)
    args = [nc.dram_tensor(f"in_{n}", arrays[n].shape, F32, kind="ExternalInput").ap() for n in _ORDER]
    out = nc.dram_tensor("out", [TOKENS, D], F32, kind="ExternalOutput").ap()
    build(nc, *args, out)
    r = run_bass_kernel_spmd(nc, [{f"in_{n}": np.ascontiguousarray(arrays[n]) for n in _ORDER}], core_ids=[0])
    return r.results[0]["out"].reshape(BATCHES, SEQ, D)
```
